# Optimizing a Trainium2 kernel written in Bass

```python
import numpy as np
import jax
import jax.numpy as jnp

def _softmax(x, axis=-1):
    return jax.nn.softmax(x, axis=axis)

def _gelu(x):
    return jax.nn.gelu(x, approximate=True)

def _silu(x):
    return jax.nn.silu(x)

def _sigmoid(x):
    return jax.nn.sigmoid(x)

def _layernorm(x, axis=-1, eps=1e-05):
    m = jnp.mean(x, axis=axis, keepdims=True)
    v = jnp.var(x, axis=axis, keepdims=True)
    return (x - m) / jnp.sqrt(v + eps)

def _scatter_add(tgt, idx, src, axis=0):
    return tgt.at[idx].add(src)

def _segment_sum(src, seg, n):
    return jax.ops.segment_sum(src, seg, n)
kernel_name = 'mk_dlrm_tower_d1_rec_r8_03b613'

def setup_inputs(seed: int=0):
    np.random.seed(seed)
    _w = jnp.asarray

    def _rec_inputs():
        import jax
        import jax.numpy as jnp
        _tk = jax.random.key(seed)
        ids = jnp.stack([jax.random.randint(jax.random.fold_in(_tk, 200 + f), (2048,), 0, v, jnp.int32) for f, v in enumerate([12500, 12500, 125000, 1000, 12500, 12500, 12500, 1250, 12500, 1250, 1250, 12500, 1000, 1000, 1000, 1250, 1000, 1000, 1000, 1000, 1000, 1250, 1250, 1250, 12500, 1250])], axis=1)
        tbl_0 = 0.05 * jax.random.normal(jax.random.fold_in(_tk, 500 + 0), (12500, 128), jnp.float32)
        tbl_1 = 0.05 * jax.random.normal(jax.random.fold_in(_tk, 500 + 1), (12500, 128), jnp.float32)
        tbl_2 = 0.05 * jax.random.normal(jax.random.fold_in(_tk, 500 + 2), (125000, 128), jnp.float32)
        tbl_3 = 0.05 * jax.random.normal(jax.random.fold_in(_tk, 500 + 3), (1000, 128), jnp.float32)
        tbl_4 = 0.05 * jax.random.normal(jax.random.fold_in(_tk, 500 + 4), (12500, 128), jnp.float32)
        tbl_5 = 0.05 * jax.random.normal(jax.random.fold_in(_tk, 500 + 5), (12500, 128), jnp.float32)
        tbl_6 = 0.05 * jax.random.normal(jax.random.fold_in(_tk, 500 + 6), (12500, 128), jnp.float32)
        tbl_7 = 0.05 * jax.random.normal(jax.random.fold_in(_tk, 500 + 7), (1250, 128), jnp.float32)
        tbl_8 = 0.05 * jax.random.normal(jax.random.fold_in(_tk, 500 + 8), (12500, 128), jnp.float32)
        tbl_9 = 0.05 * jax.random.normal(jax.random.fold_in(_tk, 500 + 9), (1250, 128), jnp.float32)
        tbl_10 = 0.05 * jax.random.normal(jax.random.fold_in(_tk, 500 + 10), (1250, 128), jnp.float32)
        tbl_11 = 0.05 * jax.random.normal(jax.random.fold_in(_tk, 500 + 11), (12500, 128), jnp.float32)
        tbl_12 = 0.05 * jax.random.normal(jax.random.fold_in(_tk, 500 + 12), (1000, 128), jnp.float32)
        tbl_13 = 0.05 * jax.random.normal(jax.random.fold_in(_tk, 500 + 13), (1000, 128), jnp.float32)
        tbl_14 = 0.05 * jax.random.normal(jax.random.fold_in(_tk, 500 + 14), (1000, 128), jnp.float32)
        tbl_15 = 0.05 * jax.random.normal(jax.random.fold_in(_tk, 500 + 15), (1250, 128), jnp.float32)
        tbl_16 = 0.05 * jax.random.normal(jax.random.fold_in(_tk, 500 + 16), (1000, 128), jnp.float32)
        tbl_17 = 0.05 * jax.random.normal(jax.random.fold_in(_tk, 500 + 17), (1000, 128), jnp.float32)
        tbl_18 = 0.05 * jax.random.normal(jax.random.fold_in(_tk, 500 + 18), (1000, 128), jnp.float32)
        tbl_19 = 0.05 * jax.random.normal(jax.random.fold_in(_tk, 500 + 19), (1000, 128), jnp.float32)
        tbl_20 = 0.05 * jax.random.normal(jax.random.fold_in(_tk, 500 + 20), (1000, 128), jnp.float32)
        tbl_21 = 0.05 * jax.random.normal(jax.random.fold_in(_tk, 500 + 21), (1250, 128), jnp.float32)
        tbl_22 = 0.05 * jax.random.normal(jax.random.fold_in(_tk, 500 + 22), (1250, 128), jnp.float32)
        tbl_23 = 0.05 * jax.random.normal(jax.random.fold_in(_tk, 500 + 23), (1250, 128), jnp.float32)
        tbl_24 = 0.05 * jax.random.normal(jax.random.fold_in(_tk, 500 + 24), (12500, 128), jnp.float32)
        tbl_25 = 0.05 * jax.random.normal(jax.random.fold_in(_tk, 500 + 25), (1250, 128), jnp.float32)
        _rk = jax.random.fold_in(_tk, 7)
        r_dense_proj = -0.000520686 + 1.00062 * jax.random.normal(jax.random.fold_in(_rk, 101), (2048, 128), jnp.float32)
        W_top1 = 0.0405887 * jax.random.normal(jax.random.fold_in(_tk, 801), (607, 512), jnp.float32)
        W_top2 = 0.0441942 * jax.random.normal(jax.random.fold_in(_tk, 802), (512, 256), jnp.float32)
        W_top3 = 0.0625 * jax.random.normal(jax.random.fold_in(_tk, 803), (256, 1), jnp.float32)
        b_top1 = jnp.zeros((512,), jnp.float32)
        b_top2 = jnp.zeros((256,), jnp.float32)
        return (r_dense_proj, ids, tbl_0, tbl_1, tbl_2, tbl_3, tbl_4, tbl_5, tbl_6, tbl_7, tbl_8, tbl_9, tbl_10, tbl_11, tbl_12, tbl_13, tbl_14, tbl_15, tbl_16, tbl_17, tbl_18, tbl_19, tbl_20, tbl_21, tbl_22, tbl_23, tbl_24, tbl_25, W_top1, b_top1, W_top2, b_top2, W_top3)
    r_dense_proj, ids, tbl_0, tbl_1, tbl_2, tbl_3, tbl_4, tbl_5, tbl_6, tbl_7, tbl_8, tbl_9, tbl_10, tbl_11, tbl_12, tbl_13, tbl_14, tbl_15, tbl_16, tbl_17, tbl_18, tbl_19, tbl_20, tbl_21, tbl_22, tbl_23, tbl_24, tbl_25, W_top1, b_top1, W_top2, b_top2, W_top3 = _rec_inputs()

    def _L0_rec_setup():
        import jax, jax.numpy as jnp
        import numpy as np
        key = jax.random.key(seed)
        k1, k2 = jax.random.split(key)
        B, N_SPARSE, D = (2048, 26, 128)
        dense_proj = jax.random.normal(k1, (B, D), dtype=jnp.float32)
        sparse_embs = jax.random.normal(k2, (B, N_SPARSE, D), dtype=jnp.float32)
        return {'dense_proj': dense_proj, 'sparse_embs': sparse_embs}
    _L0_rec_all = _L0_rec_setup()
    _L0_rec_in = {k: v for k, v in _L0_rec_all.items() if k in ()}
    del _L0_rec_all
    return {'r_dense_proj': r_dense_proj, 'ids': ids, 'tbl_0': tbl_0, 'tbl_1': tbl_1, 'tbl_2': tbl_2, 'tbl_3': tbl_3, 'tbl_4': tbl_4, 'tbl_5': tbl_5, 'tbl_6': tbl_6, 'tbl_7': tbl_7, 'tbl_8': tbl_8, 'tbl_9': tbl_9, 'tbl_10': tbl_10, 'tbl_11': tbl_11, 'tbl_12': tbl_12, 'tbl_13': tbl_13, 'tbl_14': tbl_14, 'tbl_15': tbl_15, 'tbl_16': tbl_16, 'tbl_17': tbl_17, 'tbl_18': tbl_18, 'tbl_19': tbl_19, 'tbl_20': tbl_20, 'tbl_21': tbl_21, 'tbl_22': tbl_22, 'tbl_23': tbl_23, 'tbl_24': tbl_24, 'tbl_25': tbl_25, 'W_top1': W_top1, 'b_top1': b_top1, 'W_top2': W_top2, 'b_top2': b_top2, 'W_top3': W_top3}

def reference(r_dense_proj, ids, tbl_0, tbl_1, tbl_2, tbl_3, tbl_4, tbl_5, tbl_6, tbl_7, tbl_8, tbl_9, tbl_10, tbl_11, tbl_12, tbl_13, tbl_14, tbl_15, tbl_16, tbl_17, tbl_18, tbl_19, tbl_20, tbl_21, tbl_22, tbl_23, tbl_24, tbl_25, W_top1, b_top1, W_top2, b_top2, W_top3):
    import jax
    import jax.numpy as jnp

    def _L0_rec_ref(dense_proj, sparse_embs):
        import jax, jax.numpy as jnp
        import numpy as np
        all_vecs = jnp.concatenate([dense_proj[:, None, :], sparse_embs], axis=1)
        n = all_vecs.shape[1]
        interactions = jnp.einsum('bnd,bmd->bnm', all_vecs, all_vecs)
        rows, cols = np.triu_indices(n, k=1)
        interact_flat = interactions[:, rows, cols]
        return jnp.concatenate([dense_proj, interact_flat], axis=1)
    e = jnp.stack([tbl_0[ids[:, 0]], tbl_1[ids[:, 1]], tbl_2[ids[:, 2]], tbl_3[ids[:, 3]], tbl_4[ids[:, 4]], tbl_5[ids[:, 5]], tbl_6[ids[:, 6]], tbl_7[ids[:, 7]], tbl_8[ids[:, 8]], tbl_9[ids[:, 9]], tbl_10[ids[:, 10]], tbl_11[ids[:, 11]], tbl_12[ids[:, 12]], tbl_13[ids[:, 13]], tbl_14[ids[:, 14]], tbl_15[ids[:, 15]], tbl_16[ids[:, 16]], tbl_17[ids[:, 17]], tbl_18[ids[:, 18]], tbl_19[ids[:, 19]], tbl_20[ids[:, 20]], tbl_21[ids[:, 21]], tbl_22[ids[:, 22]], tbl_23[ids[:, 23]], tbl_24[ids[:, 24]], tbl_25[ids[:, 25]]], axis=1)
    z = _L0_rec_ref(r_dense_proj, e)
    z = z.reshape(z.shape[0], -1)
    h = jnp.concatenate([z, r_dense_proj], axis=1)
    h = jnp.maximum(h @ W_top1 + b_top1, 0.0)
    h = jnp.maximum(h @ W_top2 + b_top2, 0.0)
    y = h @ W_top3
    return y

_drawn_inputs = setup_inputs


def setup_inputs(seed=0):
    import zlib

    import numpy as np

    out = dict(_drawn_inputs(seed))
    spreads = {'b_top1': (0.0, 0.1), 'b_top2': (0.0, 0.1)}
    factors = {}
    for name, (base, spread) in spreads.items():
        noise = np.random.default_rng([zlib.crc32(name.encode()), seed]).standard_normal(out[name].shape)
        drawn = base * np.exp(spread * noise) if base else spread * noise
        out[name] = jnp.asarray(drawn.astype(out[name].dtype))
    for name, factor in factors.items():
        out[name] = (out[name] * factor).astype(out[name].dtype)
    return out
```

```python
import concourse.bass as bass
from concourse import mybir
from contextlib import ExitStack

P = 128
TABLE_ROWS = [12500, 12500, 125000, 1000, 12500, 12500, 12500, 1250, 12500, 1250, 1250, 12500, 1000,
              1000, 1000, 1250, 1000, 1000, 1000, 1000, 1000, 1250, 1250, 1250, 12500, 1250]
BATCH, D, H1, H2 = 2048, 128, 512, 256
FEATURES = len(TABLE_ROWS)
VECS = FEATURES + 1
TILES = BATCH // P
PAIRS = TILES // 2
COLS = 2 * P

SELECTED = [4, 13, 14, 15, 17, 18, 19, 20]
SELECT_ROWS = 1000
CHUNKS = 8
SEL_P = SELECT_ROWS // CHUNKS
NSEL = len(SELECTED)
RAW_SLOTS = 6
BANKS_SEL = NSEL // 2
GROUPS = [(1, 1, 3), (5, 1, 4), (9, 1, 4), (22, 1, 4), (16, 5, 3)]
NGROUPS = len(GROUPS)
SLOT_OF_GROUP = [sum(n for _, _, n in GROUPS[:g]) for g in range(NGROUPS)]
NGATHER = sum(n for _, _, n in GROUPS)

N_PER = VECS - 1
RECTANGLES = [[(0, 8, 11, 27)],
              [(8, 17, 17, 27), (0, 4, 4, 11), (0, 3, 1, 4)],
              [(17, 22, 22, 27), (8, 12, 12, 17), (4, 8, 8, 11), (4, 7, 5, 8), (8, 11, 9, 12),
               (12, 16, 13, 17), (17, 21, 18, 22), (22, 26, 23, 27)]]
PLACED = []
CHUNK_SIZES = []
for _k, _rectangles in enumerate(RECTANGLES):
    _row = 0
    for _n0, _n1, _m0, _m1 in _rectangles:
        PLACED.append((_k, _row, (_n0, _n1, _m0, _m1)))
        _row += (_n1 - _n0) * (_m1 - _m0)
    CHUNK_SIZES.append(_row)
NPAIRCHUNKS = len(CHUNK_SIZES)
PACKS = 16 * len(PLACED)
HC1, HC2 = H1 // P, H2 // P
GRAM_ROWS = 16

USES = ["select0", "select1", "select2", "select3",
        "hidden1_0", "hidden1_1", "hidden1_2", "hidden1_3", "hidden2_0", "hidden2_1", "out0", "out1"]
STEPS = ["select0", "group00", "select1", "group01", "select2", "group02", "group03", "select3", "group04",
         "hidden1_0", "products00", "hidden1_1", "products01", "group10", "group11", "hidden1_2", "group12",
         "hidden1_3", "hidden2_0", "group13", "group14", "hidden2_1", "products10", "out0", "out1", "products11"]
MLP_USES = HC1 + HC2 + 2
TILE_USES = HC1 + HC2 + 1


def pair_row(n, m):
    return D + n * N_PER - n * (n - 1) // 2 + (m - n - 1)


def weight_rows():
    for k, row, (n0, n1, m0, m1) in PLACED:
        for n in range(n0, n1):
            m = max(m0, n + 1)
            yield k, row + (n - n0) * (m1 - m0) + (m - m0), pair_row(n, m), m1 - m


def dlrm_tower(nc, dense, ids, tables, w1, b1, w2, b2, w3, out):
    f32, f32r, i32 = mybir.dt.float32, mybir.dt.float32r, mybir.dt.int32
    ALU = mybir.AluOpType
    ACT = mybir.ActivationFunctionType
    ctx = ExitStack()
    with ctx:
        def sb(name, shape, dt=f32):
            return ctx.enter_context(nc.sbuf_tensor(name, shape, dt))

        def bank(name):
            return ctx.enter_context(nc.psum_tensor(name, [P, 512], f32))

        def sem(name):
            return ctx.enter_context(nc.semaphore(name))

        ident = sb("ident", [P, P])
        row_number_i = sb("row_number_i", [P, CHUNKS], i32)
        row_number = sb("row_number", [P, CHUNKS])
        spread_sel = sb("spread_sel", [P, NSEL, P], f32r)
        ids_all = sb("ids_all", [P, TILES, FEATURES], i32)
        ids_f = sb("ids_f", [P, TILES, FEATURES])
        ids_t = sb("ids_t", [P, BATCH], f32r)
        ids_spread = sb("ids_spread", [P, 2, 2 * COLS])
        gather_ids = sb("gather_ids", [P, 2, FEATURES], i32)
        gathered = sb("gathered", [P, 2, NGATHER, D])
        dense_t = sb("dense_t", [P, BATCH])
        table_hi = sb("table_hi", [P, NSEL, CHUNKS * D], f32r)
        table_lo = sb("table_lo", [P, NSEL, CHUNKS * D], f32r)
        onehot = sb("onehot", [P, 2, CHUNKS, COLS], f32r)
        vecs = sb("vecs", [P, COLS, VECS])
        dense_rows = vecs[:, :, :].rearrange("p b n -> p (b n)")[:, 0:TILES * D].rearrange("p (t d) -> p t d", d=D)
        products_all = sb("products", [P, 2, N_PER, P])
        products = products_all[0:N_PER, :, :, :]
        table_raw = products_all[:, :, :, :].rearrange("p s m b -> p (s m b)")[:, 0:RAW_SLOTS * CHUNKS * D] \
            .rearrange("p (k d) -> p k d", k=RAW_SLOTS)
        packed = sb("packed", [P, NPAIRCHUNKS, COLS])
        w1_dense = sb("w1_dense", [P, H1])
        w1_tail = sb("w1_tail", [P, H1])
        w1_pairs = sb("w1_pairs", [P, NPAIRCHUNKS, H1])
        w2_sb = sb("w2_sb", [P, HC1, H2])
        small_rows = sb("small_rows", [HC1 + 2 * HC2, P])
        small = sb("small", [P, HC1 + 2 * HC2])
        hidden1 = sb("hidden1", [P, HC1, COLS])
        hidden2 = sb("hidden2", [P, HC2, COLS])
        y = sb("y", [P, TILES])

        bank_t = [bank(f"bank_t{k}") for k in range(2)]
        bank_g = [bank(f"bank_g{k}") for k in range(2)]
        bank_s = [bank(f"bank_s{k}") for k in range(2)]
        bank_m = [bank(f"bank_m{k}") for k in range(2)]

        s_ident0, s_ident, s_iota, s_consts = sem("s_ident0"), sem("s_ident"), sem("s_iota"), sem("s_consts")
        s_ids, s_dense, s_small = sem("s_ids"), sem("s_dense"), sem("s_small")
        s_raw = [sem(f"s_raw{k}") for k in range(RAW_SLOTS)]
        s_w1d, s_w = sem("s_w1d"), sem("s_w")
        s_ids_f = sem("s_ids_f")
        s_zero = sem("s_zero")
        s_setup = sem("s_setup")
        s_setup_act, s_setup_dve = sem("s_setup_act"), sem("s_setup_dve")
        s_hi, s_lo = sem("s_hi"), sem("s_lo")
        s_w1sum = sem("s_w1sum")
        s_refill = sem("s_refill")
        s_gids = sem("s_gids")
        s_gath = [[sem(f"s_gath{s}_{g}") for g in range(NGROUPS)] for s in range(2)]
        s_spread = sem("s_spread")
        s_spread_sb = sem("s_spread_sb")
        s_onehot = sem("s_onehot")
        s_sel = sem("s_sel")
        s_t = sem("s_t")
        s_t_act, s_t_dve = sem("s_t_act"), sem("s_t_dve")
        s_g = sem("s_g")
        s_g_act, s_g_dve = sem("s_g_act"), sem("s_g_dve")
        s_pack = [sem(f"s_pack{s}") for s in range(2)]
        s_mlp = sem("s_mlp")
        s_m_act = sem("s_m_act")
        s_out = sem("s_out")

        block = ctx.enter_context(nc.Block())

        def use_of(i, what):
            if isinstance(i, int) and i == 0:
                return int(what[-1])
            return i * len(USES) + (USES.index(what) - MLP_USES)

        def bank_of(i, what):
            first = isinstance(i, int) and i == 0
            return bank_m[(int(what[-1]) if first else USES.index(what)) % 2]

        LAST_USE = len(USES) * PAIRS - MLP_USES

        def cols_of(s):
            return slice(s * P, (s + 1) * P)

        @block.sync
        def _(sp):
            sp.dma_start(ids_all[:, :, :], ids.rearrange("(p t) f -> p t f", t=TILES)).then_inc(s_ids, 16)

            def load_table(k):
                src = tables[SELECTED[k] - 1].rearrange("(p c) d -> p (c d)", c=CHUNKS)
                if k >= RAW_SLOTS:
                    sp.wait_ge(s_hi, k - RAW_SLOTS + 1)
                    sp.wait_ge(s_lo, k - RAW_SLOTS + 1)
                lead = SEL_P // 16 * 16
                sp.dma_start(table_raw[0:lead, k % RAW_SLOTS, :], src[0:lead, :]).then_inc(s_raw[k % RAW_SLOTS], 16)
                sp.dma_start(table_raw[lead:SEL_P, k % RAW_SLOTS, :], src[lead:SEL_P, :]).then_inc(s_raw[k % RAW_SLOTS], 16)

            for k in range(NSEL):
                load_table(k)
            sp.dma_start(w1_dense[:, :], w1[0:D, :]).then_inc(s_w1d, 16)
            sp.dma_start(w1_tail[:, :], w1[D + VECS * N_PER // 2:, :]).then_inc(s_w1d, 16)
            sp.dma_start(w2_sb[:, :, :], w2.rearrange("(k p) n -> p k n", p=P)).then_inc(s_w, 16)
            sp.wait_ge(s_zero, 1)
            for k, row, at, count in weight_rows():
                sp.dma_start(w1_pairs[row:row + count, k, :], w1[at:at + count, :]).then_inc(s_w, 16)

            def pack(i, s, first):
                t = i * 2 + s
                sp.wait_ge(s_g_act, t + 1)
                sp.wait_ge(s_g_dve, t + 1)
                if not first:
                    sp.wait_ge(s_mlp, i * MLP_USES + (HC1 - MLP_USES))
                for k, row, (n0, n1, m0, m1) in PLACED:
                    sp.dma_start(packed[row:row + (n1 - n0) * (m1 - m0), k, cols_of(s)],
                                 products[n0:n1, s, m0 - 1:m1 - 1, :]).then_inc(s_pack[s], 16)

            for s in range(2):
                pack(0, s, True)
            with sp.Fori(1, PAIRS) as i:
                for s in range(2):
                    pack(i, s, False)
            sp.wait_ge(s_m_act, LAST_USE + 2 * TILE_USES)
            sp.dma_start(out.rearrange("(p t) o -> p (t o)", t=TILES), y[:, :]).then_inc(s_out, 16)
            sp.wait_ge(s_out, 16)

        @block.gpsimd
        def _(pool):
            pool.memset(ident[:, :], 0.0).then_inc(s_ident0, 1)
            pool.iota(row_number_i[:, :], pattern=[[1, CHUNKS]], base=0, channel_multiplier=CHUNKS).then_inc(s_iota, 1)
            pool.wait_ge(s_ident0, 1)
            pool.affine_select(out=ident[:, :], in_=ident[:, :], compare_op=ALU.not_equal, fill=1.0,
                               base=0, pattern=[[-1, P]], channel_multiplier=1).then_inc(s_ident, 1)
            pool.wait_ge(s_ids, 16)
            pool.tensor_copy(gather_ids[:, 0, :], ids_all[:, 0, :]).then_inc(s_gids, 1)

            def gather_tile(i, s, first, last):
                t = i * 2 + s
                pool.wait_ge(s_gids, t + 1)
                for g, (n0, step, count) in enumerate(GROUPS):
                    if not first:
                        pool.wait_ge(s_t, t * NGROUPS + (g + 1 - 2 * NGROUPS))
                        pool.sem_inc(s_refill, 1)
                    for j in range(count):
                        f = n0 + j * step - 1
                        pool.indirect_dma_start(
                            out=gathered[:, s, SLOT_OF_GROUP[g] + j, :], out_offset=None, in_=tables[f][:, :],
                            in_offset=bass.IndirectOffsetOnAxis(ap=gather_ids[:, s, f:f + 1], axis=0),
                            bounds_check=TABLE_ROWS[f] - 1, oob_is_err=False).then_inc(s_gath[s][g], 16)
                    if g == 1 and not (last and s == 1):
                        if not (first and s == 0):
                            for h in range(NGROUPS):
                                pool.wait_ge(s_gath[1 - s][h], (i + s) * (16 * GROUPS[h][2]))
                        pool.wait_ge(s_ids, 16)
                        nxt = ids_all[:, t + 1, :] if first or last else \
                            ids_all[:, bass.ds(t + 1, 1), :].rearrange("p a f -> p (a f)")
                        pool.tensor_copy(gather_ids[:, 1 - s, :], nxt).then_inc(s_gids, 1)

            def gather_pair(i, first, last):
                for s in range(2):
                    gather_tile(i, s, first, last)

            gather_pair(0, True, False)
            with pool.Fori(1, PAIRS - 1) as i:
                gather_pair(i, False, False)
            gather_pair(PAIRS - 1, False, True)

        @block.tensor
        def _(pe):
            def setup_round(r, parts):
                if r >= 2:
                    pe.wait_ge((s_setup_act, s_setup_dve)[r % 2], r // 2)
                for dst, src, idn in parts:
                    last = nc.tensor.transpose(dst, src, idn)
                last.then_inc(s_setup, 1)

            pe.wait_ge(s_ident, 1)
            pe.wait_ge(s_ids_f, 1)
            for r in range(4):
                setup_round(r, [(bank_t[r % 2][0:FEATURES, q * P:(q + 1) * P], ids_f[:, 4 * r + q, :], ident[:, :])
                                for q in range(4)])

            def spread(i, q):
                if isinstance(i, int) and 4 * i + q < 2:
                    pass
                else:
                    pe.wait_ge(s_spread_sb, i * BANKS_SEL + (q - 1))
                if isinstance(i, int):
                    moving = ids_t[:, i * COLS:(i + 1) * COLS]
                else:
                    moving = ids_t[:, bass.ds(i * COLS, COLS)]
                for h in range(2):
                    last = nc.tensor.matmul(bank_s[q % 2][:, h * COLS:(h + 1) * COLS],
                                            spread_sel[:, 2 * q + h, :], moving, start=True, stop=True)
                last.then_inc(s_spread, 1)

            def select(i, q, first):
                what = f"select{q}"
                if not first or q >= 2:
                    pe.wait_ge(s_m_act, use_of(i, what) - 1)
                for h in range(2):
                    k = 2 * q + h
                    pe.wait_ge(s_onehot, i * NSEL + (k + 1))
                    if first:
                        pe.wait_ge(s_hi, k + 1)
                        pe.wait_ge(s_lo, k + 1)
                    for part in (table_hi, table_lo):
                        for c in range(CHUNKS):
                            last = nc.tensor.matmul(bank_of(i, what)[:, h * COLS:(h + 1) * COLS],
                                                    part[0:SEL_P, k, c * D:(c + 1) * D],
                                                    onehot[0:SEL_P, k % 2, c, :],
                                                    start=part is table_hi and c == 0,
                                                    stop=part is table_lo and c == CHUNKS - 1)
                    last.then_inc(s_sel, 1)

            def hidden1_part(c, dst, dense_cols, cols):
                nc.tensor.matmul(dst, w1_dense[:, c * P:(c + 1) * P], dense_cols, start=True, stop=False)
                for k, rows in enumerate(CHUNK_SIZES):
                    last = nc.tensor.matmul(dst, w1_pairs[0:rows, k, c * P:(c + 1) * P], packed[0:rows, k, cols],
                                            start=False, stop=k == NPAIRCHUNKS - 1)
                last.then_inc(s_mlp, 1)

            def hidden2_part(c, dst, cols, stored):
                for k in range(HC1):
                    if c == 0:
                        pe.wait_ge(s_m_act, stored(k))
                    last = nc.tensor.matmul(dst, w2_sb[:, k, c * P:(c + 1) * P], hidden1[:, k, cols],
                                            start=k == 0, stop=k == HC1 - 1)
                last.then_inc(s_mlp, 1)

            def out_part(s, dst):
                for k in range(HC2):
                    col = HC1 + HC2 + k
                    last = nc.tensor.matmul(dst, hidden2[:, k, cols_of(s)], small[:, col:col + 1],
                                            start=k == 0, stop=k == HC2 - 1)
                last.then_inc(s_mlp, 1)

            def tower_step(i, what):
                use = use_of(i, what)
                kind, c = what[:-1], int(what[-1])
                dst = bank_of(i, what)
                if what == "hidden1_0":
                    for s in range(2):
                        pe.wait_ge(s_pack[s], i * PACKS)
                if what == "out0":
                    pe.wait_ge(s_m_act, use_of(i, "hidden2_1") + 1)
                else:
                    pe.wait_ge(s_m_act, use - 1)
                if kind == "hidden1_":
                    if isinstance(i, int):
                        dense_cols = dense_t[:, (i - 1) * COLS:i * COLS]
                    else:
                        dense_cols = dense_t[:, bass.ds(i * COLS - COLS, COLS)]
                    hidden1_part(c, dst[:, 0:COLS], dense_cols, slice(0, COLS))
                elif kind == "hidden2_":
                    hidden2_part(c, dst[:, 0:COLS], slice(0, COLS), lambda k: use_of(i, f"hidden1_{k}") + 1)
                else:
                    out_part(c, dst[:, 0:1])

            def last_tower(s):
                use = LAST_USE + s * TILE_USES
                t = TILES - 2 + s
                pe.wait_ge(s_pack[s], PAIRS * PACKS)
                for c in range(HC1):
                    pe.wait_ge(s_m_act, use + c - 1)
                    hidden1_part(c, bank_m[(use + c) % 2][:, 0:P], dense_t[:, t * P:(t + 1) * P], cols_of(s))
                for c in range(HC2):
                    if c:
                        pe.wait_ge(s_m_act, use + HC1 + c - 1)
                    hidden2_part(c, bank_m[(use + HC1 + c) % 2][:, 0:P], cols_of(s),
                                 lambda k: use + max(k, HC1 - 2) + 1)
                pe.wait_ge(s_m_act, use + HC1 + HC2)
                out_part(s, bank_m[(use + HC1 + HC2) % 2][:, 0:1])

            def transpose_group(i, s, g, first):
                count = GROUPS[g][2]
                u = s * NGROUPS + g
                if first and u < 2:
                    pe.wait_ge((s_setup_act, s_setup_dve)[u % 2], (5, 4)[u % 2])
                else:
                    pe.wait_ge((s_t_act, s_t_dve)[u % 2], i * NGROUPS + u // 2)
                pe.wait_ge(s_gath[s][g], i * (16 * count) + 16 * count)
                for j in range(count):
                    last = nc.tensor.transpose(bank_t[u % 2][:, j * P:(j + 1) * P],
                                               gathered[:, s, SLOT_OF_GROUP[g] + j, :], ident[:, :])
                last.then_inc(s_t, 1)

            def multiply_half(i, s, h, first):
                if h == 0:
                    pe.wait_ge(s_t_act, i * NGROUPS + (3, 5)[s])
                    pe.wait_ge(s_t_dve, i * NGROUPS + (2, 5)[s])
                    if s == 0:
                        pe.wait_ge(s_m_act, use_of(i, "select3") + 1)
                if not (first and s == 0):
                    pe.wait_ge((s_g_act, s_g_dve)[h], i * 2 + s)
                for r in range(GRAM_ROWS):
                    for j in range(4):
                        b = s * P + h * 64 + j * GRAM_ROWS + r
                        last = nc.tensor.matmul(
                            bank_g[h][32 * j:32 * j + N_PER, r * N_PER:(r + 1) * N_PER],
                            vecs[:, b, 0:N_PER], vecs[:, b, 1:VECS], start=True, stop=True)
                last.then_inc(s_g, 1)

            def iteration(i, first, last):
                for step in STEPS:
                    if step.startswith("select"):
                        q = int(step[-1])
                        if q + 1 < BANKS_SEL:
                            spread(i, q + 1)
                        elif not last:
                            spread(i + 1, 0)
                        select(i, q, first)
                    elif step.startswith("group"):
                        transpose_group(i, int(step[-2]), int(step[-1]), first)
                    elif step.startswith("products"):
                        multiply_half(i, int(step[-2]), int(step[-1]), first)
                    elif not first:
                        tower_step(i, step)

            pe.wait_ge(s_consts, 1)
            pe.wait_ge(s_setup_act, 2)
            pe.wait_ge(s_setup_dve, 2)
            spread(0, 0)
            pe.wait_ge(s_dense, 16)
            for r in range(4, 8):
                setup_round(r, [(bank_t[r % 2][:, q * P:(q + 1) * P], dense_rows[:, 4 * (r - 4) + q, :], ident[:, :])
                                for q in range(4)])
            pe.wait_ge(s_small, 48)
            ns = HC1 + 2 * HC2
            setup_round(8, [(bank_t[0][:, 0:ns], small_rows[:, :], ident[0:ns, 0:ns])])
            iteration(0, True, False)
            pe.wait_ge(s_w, 16 * (len(list(weight_rows())) + 1))
            pe.wait_ge(s_w1sum, 1)
            with pe.Fori(1, PAIRS - 1) as i:
                iteration(i, False, False)
            iteration(PAIRS - 1, False, True)
            last_tower(0)
            last_tower(1)

        @block.scalar
        def _(act):
            act.dma_start(dense_rows[:, :, :], dense.rearrange("(p t) d -> p t d", t=TILES)).then_inc(s_dense, 16)
            act.dma_start(small_rows[0:HC1, :], b1.rearrange("(c p) -> c p", p=P)).then_inc(s_small, 16)
            act.dma_start(small_rows[HC1:HC1 + HC2, :], b2.rearrange("(c p) -> c p", p=P)).then_inc(s_small, 16)
            act.dma_start(small_rows[HC1 + HC2:HC1 + 2 * HC2, :],
                          w3.rearrange("(c p) o -> c (p o)", p=P)).then_inc(s_small, 16)

            def store(dst, src):
                return nc.scalar.activation(dst, src, ACT.Copy)

            act.wait_ge(s_zero, 1)
            for r in (0, 2):
                act.wait_ge(s_setup, r + 1)
                store(ids_t[0:FEATURES, r * 512:(r + 1) * 512], bank_t[0][0:FEATURES, :]).then_inc(s_setup_act, 1)

            def store_spread(i, q):
                if not (isinstance(i, int) and 4 * i + q < 2):
                    act.wait_ge(s_onehot, i * NSEL + (2 * q - 2))
                act.wait_ge(s_spread, i * BANKS_SEL + (q + 1))
                store(ids_spread[:, q % 2, :], bank_s[q % 2][:, :]).then_inc(s_spread_sb, 1)

            def split_hi(k):
                act.wait_ge(s_raw[k % RAW_SLOTS], 32 * (k // RAW_SLOTS + 1))
                store(table_hi[0:SEL_P, k, :], table_raw[0:SEL_P, k % RAW_SLOTS, :]).then_inc(s_hi, 1)

            def store_selected(i, q):
                act.wait_ge(s_sel, i * NSEL + (2 * q + 2))
                a, b = SELECTED[2 * q], SELECTED[2 * q + 1]
                store(vecs[:, :, a:b + 1:b - a].rearrange("p b k -> p k b"),
                      bank_of(i, f"select{q}")[:, :].rearrange("p (k b) -> p k b", k=2)).then_inc(s_m_act, 1)

            def relu(dst, src, col):
                nc.scalar.activation(dst, src, ACT.Relu, bias=small[:, col:col + 1]).then_inc(s_m_act, 1)

            def tower_step(i, what):
                c = int(what[-1])
                src = bank_of(i, what)
                at = [w for w in USES if not w.startswith("select")].index(what)
                act.wait_ge(s_mlp, i * MLP_USES + (at + 1 - MLP_USES))
                if what.startswith("hidden1"):
                    relu(hidden1[:, c, :], src[:, 0:COLS], c)
                elif what.startswith("hidden2"):
                    relu(hidden2[:, c, :], src[:, 0:COLS], HC1 + c)
                else:
                    dst = y[:, 2 * i - 2 + c:2 * i - 1 + c] if isinstance(i, int) else y[:, bass.ds(2 * i + (c - 2), 1)]
                    store(dst, src[:, 0:1]).then_inc(s_m_act, 1)

            def last_tower(s):
                use = LAST_USE + s * TILE_USES
                done = (PAIRS - 1) * MLP_USES + s * TILE_USES
                for c in range(HC1):
                    act.wait_ge(s_mlp, done + c + 1)
                    relu(hidden1[:, c, cols_of(s)], bank_m[(use + c) % 2][:, 0:P], c)
                for c in range(HC2):
                    act.wait_ge(s_mlp, done + HC1 + c + 1)
                    relu(hidden2[:, c, cols_of(s)], bank_m[(use + HC1 + c) % 2][:, 0:P], HC1 + c)
                act.wait_ge(s_mlp, done + TILE_USES)
                t = TILES - 2 + s
                store(y[:, t:t + 1], bank_m[(use + HC1 + HC2) % 2][:, 0:1]).then_inc(s_m_act, 1)

            def store_group(i, s, g):
                u = s * NGROUPS + g
                n0, step, count = GROUPS[g]
                act.wait_ge(s_t, i * (2 * NGROUPS) + (u + 1))
                if g == 0:
                    store_dense(i, s)
                store(vecs[:, cols_of(s), n0:n0 + step * (count - 1) + 1:step].rearrange("p b n -> p n b"),
                      bank_t[0][:, 0:count * P].rearrange("p (n b) -> p n b", n=count)).then_inc(s_t_act, 1)

            def store_dense(i, s):
                if isinstance(i, int):
                    src = dense_t[:, (2 * i + s) * P:(2 * i + s + 1) * P]
                else:
                    src = dense_t[:, bass.ds(i * COLS + s * P, P)]
                store(vecs[:, cols_of(s), 0], src)

            def store_products(i, s, first):
                if not first:
                    act.wait_ge(s_pack[s], i * PACKS)
                act.wait_ge(s_g, i * 4 + (2 * s + 1))
                for j in range(4):
                    last = store(products[:, s, :, j * GRAM_ROWS:(j + 1) * GRAM_ROWS],
                                 bank_g[0][32 * j:32 * j + N_PER, 0:GRAM_ROWS * N_PER]
                                 .rearrange("p (r m) -> p m r", r=GRAM_ROWS))
                last.then_inc(s_g_act, 1)

            def iteration(i, first, last):
                for step in STEPS:
                    if step.startswith("select"):
                        q = int(step[-1])
                        if q + 1 < BANKS_SEL:
                            if first:
                                split_hi(2 * q + 2)
                                split_hi(2 * q + 3)
                            store_spread(i, q + 1)
                        elif not last:
                            store_spread(i + 1, 0)
                        store_selected(i, q)
                    elif step.startswith("group"):
                        s, g = int(step[-2]), int(step[-1])
                        if (s * NGROUPS + g) % 2 == 0:
                            store_group(i, s, g)
                    elif step.startswith("products"):
                        if step[-1] == "0":
                            store_products(i, int(step[-2]), first)
                    elif not first:
                        tower_step(i, step)

            store_spread(0, 0)
            for r in (4, 6):
                act.wait_ge(s_setup, r + 1)
                store(dense_t[:, (r - 4) * 512:(r - 3) * 512], bank_t[0][:, :]).then_inc(s_setup_act, 1)
            act.wait_ge(s_setup, 9)
            store(small[:, :], bank_t[0][:, 0:HC1 + 2 * HC2]).then_inc(s_setup_act, 1)
            act.wait_ge(s_setup_dve, 4)
            split_hi(0)
            split_hi(1)
            iteration(0, True, False)
            with act.Fori(1, PAIRS - 1) as i:
                iteration(i, False, False)
            iteration(PAIRS - 1, False, True)
            last_tower(0)
            last_tower(1)

        @block.vector
        def _(dve):
            nc.vector.memset(ids_t[:, :].bitcast(f32), 0.0)
            nc.vector.memset(w1_pairs[:, :, :], 0.0).then_inc(s_zero, 1)
            dve.wait_ge(s_ids, 16)
            nc.vector.tensor_copy(ids_f[:, :, :], ids_all[:, :, :]).then_inc(s_ids_f, 1)
            dve.wait_ge(s_iota, 1)
            nc.vector.tensor_copy(row_number[:, :], row_number_i[:, :])
            dve.wait_ge(s_ident, 1)
            for k, n in enumerate(SELECTED):
                last = nc.vector.tensor_copy(spread_sel[:, k, :], ident[:, n - 1:n].to_broadcast([P, P]))
            last.then_inc(s_consts, 1)
            dve.wait_ge(s_zero, 1)
            for r in (1, 3):
                dve.wait_ge(s_setup, r + 1)
                nc.vector.tensor_copy(ids_t[0:FEATURES, r * 512:(r + 1) * 512], bank_t[1][0:FEATURES, :]).then_inc(s_setup_dve, 1)
            dve.wait_ge(s_consts, 1)

            def split_lo(k):
                dve.wait_ge(s_hi, k + 1)
                nc.vector.tensor_tensor(table_lo[0:SEL_P, k, :], table_raw[0:SEL_P, k % RAW_SLOTS, :],
                                        table_hi[0:SEL_P, k, :].bitcast(f32), ALU.subtract).then_inc(s_lo, 1)

            def build_onehot(i, k):
                dve.wait_ge(s_spread_sb, i * BANKS_SEL + (k // 2 + 1))
                if not (isinstance(i, int) and NSEL * i + k < 2):
                    dve.wait_ge(s_sel, i * NSEL + (k - 1))
                q, h = k // 2, k % 2
                for c in range(CHUNKS):
                    last = nc.vector.tensor_scalar(onehot[0:SEL_P, k % 2, c, :],
                                                   ids_spread[0:SEL_P, q % 2, h * COLS:(h + 1) * COLS],
                                                   row_number[0:SEL_P, c:c + 1], None, ALU.is_equal)
                last.then_inc(s_onehot, 1)

            def store_group(i, s, g):
                u = s * NGROUPS + g
                n0, step, count = GROUPS[g]
                dve.wait_ge(s_t, i * (2 * NGROUPS) + (u + 1))
                if g == 0:
                    if isinstance(i, int):
                        src = dense_t[:, (2 * i + s) * P:(2 * i + s + 1) * P]
                    else:
                        src = dense_t[:, bass.ds(i * COLS + s * P, P)]
                    nc.vector.tensor_copy(vecs[:, cols_of(s), 0], src)
                nc.vector.tensor_copy(
                    vecs[:, cols_of(s), n0:n0 + step * (count - 1) + 1:step].rearrange("p b n -> p n b"),
                    bank_t[1][:, 0:count * P].rearrange("p (n b) -> p n b", n=count)).then_inc(s_t_dve, 1)

            def store_products(i, s, first):
                if not first:
                    dve.wait_ge(s_pack[s], i * PACKS)
                dve.wait_ge(s_g, i * 4 + (2 * s + 2))
                for j in range(4):
                    last = nc.vector.tensor_copy(
                        products[:, s, :, 64 + j * GRAM_ROWS:64 + (j + 1) * GRAM_ROWS],
                        bank_g[1][32 * j:32 * j + N_PER, 0:GRAM_ROWS * N_PER]
                        .rearrange("p (r m) -> p m r", r=GRAM_ROWS))
                last.then_inc(s_g_dve, 1)

            def iteration(i, first, last):
                for step in STEPS:
                    if step.startswith("select"):
                        q = int(step[-1])
                        for h in range(2):
                            if q + 1 < BANKS_SEL:
                                if first:
                                    split_lo(2 * q + 2 + h)
                                build_onehot(i, 2 * q + 2 + h)
                    elif step.startswith("group"):
                        s, g = int(step[-2]), int(step[-1])
                        if (s * NGROUPS + g) % 2 == 1:
                            store_group(i, s, g)
                    elif step.startswith("products") and step[-1] == "1":
                        store_products(i, int(step[-2]), first)
                    elif step in ("hidden1_2", "hidden1_3") and not last:
                        build_onehot(i + 1, int(step[-1]) - 2)

            for r in (5, 7):
                dve.wait_ge(s_setup, r + 1)
                nc.vector.tensor_copy(dense_t[:, (r - 4) * 512:(r - 3) * 512], bank_t[1][:, :]).then_inc(s_setup_dve, 1)
            dve.wait_ge(s_setup_act, 5)
            for k in range(2):
                split_lo(k)
                build_onehot(0, k)
            iteration(0, True, False)
            dve.wait_ge(s_w1d, 32)
            nc.vector.tensor_tensor(w1_dense[:, :], w1_dense[:, :], w1_tail[:, :], ALU.add).then_inc(s_w1sum, 1)
            with dve.Fori(1, PAIRS - 1) as i:
                iteration(i, False, False)
            iteration(PAIRS - 1, False, True)


_INS = ['r_dense_proj', 'ids'] + [f'tbl_{f}' for f in range(FEATURES)] + ['W_top1', 'b_top1', 'W_top2', 'b_top2', 'W_top3']


def kernel(**inputs):
    import numpy as np
    from concourse import bacc
    from concourse.bass_utils import run_bass_kernel_spmd

    nc = bacc.Bacc("TRN2", target_bir_lowering=False, num_devices=1)
    arrays, aps = {}, {}
    for name in _INS:
        a = np.ascontiguousarray(inputs[name])
        arrays[f"in_{name}"] = a
        aps[name] = nc.dram_tensor(f"in_{name}", a.shape, mybir.dt.from_np(a.dtype), kind="ExternalInput").ap()
    out = nc.dram_tensor("out_y", (BATCH, 1), mybir.dt.float32, kind="ExternalOutput").ap()
    dlrm_tower(nc, aps['r_dense_proj'], aps['ids'], [aps[f'tbl_{f}'] for f in range(FEATURES)],
               aps['W_top1'], aps['b_top1'], aps['W_top2'], aps['b_top2'], aps['W_top3'], out)
    r = run_bass_kernel_spmd(nc, [arrays], core_ids=[0])
    return r.results[0]["out_y"]
```

```python
import concourse.bass as bass
from concourse import mybir
from contextlib import ExitStack

P = 128
TABLE_ROWS = [12500, 12500, 125000, 1000, 12500, 12500, 12500, 1250, 12500, 1250, 1250, 12500, 1000,
              1000, 1000, 1250, 1000, 1000, 1000, 1000, 1000, 1250, 1250, 1250, 12500, 1250]
BATCH, D, H1, H2 = 2048, 128, 512, 256
FEATURES = len(TABLE_ROWS)
VECS = FEATURES + 1
TILES = BATCH // P
PAIRS = TILES // 2
COLS = 2 * P

SELECTED = [4, 13, 14, 15, 17, 18, 19, 20]
SELECT_ROWS = 1000
CHUNKS = 8
SEL_P = SELECT_ROWS // CHUNKS
NSEL = len(SELECTED)
RAW_SLOTS = 6
BANKS_SEL = NSEL // 2
SEL_STEPS = BANKS_SEL * CHUNKS
GROUPS = [(1, 1, 3), (5, 1, 4), (9, 1, 4), (22, 1, 4), (16, 5, 3)]
NGROUPS = len(GROUPS)
SLOT_OF_GROUP = [sum(n for _, _, n in GROUPS[:g]) for g in range(NGROUPS)]
NGATHER = sum(n for _, _, n in GROUPS)

N_PER = VECS - 1
RECTANGLES = [[(0, 8, 11, 27)],
              [(8, 17, 17, 27), (0, 4, 4, 11), (0, 3, 1, 4)],
              [(17, 22, 22, 27), (8, 12, 12, 17), (4, 8, 8, 11), (4, 7, 5, 8), (8, 11, 9, 12),
               (12, 16, 13, 17), (17, 21, 18, 22), (22, 26, 23, 27)]]
PLACED = []
CHUNK_SIZES = []
for _k, _rectangles in enumerate(RECTANGLES):
    _row = 0
    for _n0, _n1, _m0, _m1 in _rectangles:
        PLACED.append((_k, _row, (_n0, _n1, _m0, _m1)))
        _row += (_n1 - _n0) * (_m1 - _m0)
    CHUNK_SIZES.append(_row)
NPAIRCHUNKS = len(CHUNK_SIZES)
PACKS = 16 * len(PLACED)
HC1, HC2 = H1 // P, H2 // P
GRAM_ROWS = 16

STEPS = ["select0", "group00", "select1", "group01", "select2", "group02", "hidden1_0", "select3", "group03",
         "group04", "hidden1_1", "products00", "group10", "hidden1_2", "group11", "products01", "group12",
         "group13", "group14", "hidden1_3", "products10", "hidden2_0", "products11", "hidden2_1", "out0", "out1"]
NEXT_ONEHOT = "hidden1_3"
SPREAD_AT = 25
MBANKS = 4
USES = []
for _step in STEPS:
    if _step.startswith("select"):
        USES += [f"table{2 * int(_step[-1]) + h}" for h in range(2)]
    elif _step[:5] not in ("group", "produ"):
        USES.append(_step)
MLP_USES = HC1 + HC2 + 2
TILE_USES = HC1 + HC2 + 1


def pair_row(n, m):
    return D + n * N_PER - n * (n - 1) // 2 + (m - n - 1)


def weight_rows():
    for k, row, (n0, n1, m0, m1) in PLACED:
        for n in range(n0, n1):
            m = max(m0, n + 1)
            yield k, row + (n - n0) * (m1 - m0) + (m - m0), pair_row(n, m), m1 - m


def dlrm_tower(nc, dense, ids, tables, w1, b1, w2, b2, w3, ids_scratch, out):
    f32, f32r, f16, i32 = mybir.dt.float32, mybir.dt.float32r, mybir.dt.float16, mybir.dt.int32
    ALU = mybir.AluOpType
    ACT = mybir.ActivationFunctionType
    ctx = ExitStack()
    with ctx:
        def sb(name, shape, dt=f32):
            return ctx.enter_context(nc.sbuf_tensor(name, shape, dt))

        def bank(name):
            return ctx.enter_context(nc.psum_tensor(name, [P, 512], f32))

        def sem(name):
            return ctx.enter_context(nc.semaphore(name))

        ident = sb("ident", [P, P])
        row_number_i = sb("row_number_i", [P, CHUNKS], i32)
        row_number = sb("row_number", [P, CHUNKS])
        ids_all = sb("ids_all", [P, TILES, FEATURES], i32)
        ids_sel = sb("ids_sel", [P, TILES, NSEL])
        ids_sel_t = sb("ids_sel_t", [TILES * NSEL, P], f16)
        ids_spread = sb("ids_spread", [P, 2, NSEL, P], f16)
        gather_ids = sb("gather_ids", [P, 2, FEATURES], i32)
        gathered = sb("gathered", [P, 2, NGATHER, D])
        dense_t = sb("dense_t", [P, BATCH])
        table_hi = sb("table_hi", [P, NSEL, CHUNKS * D], f32r)
        table_lo = sb("table_lo", [P, NSEL, CHUNKS * D], f32r)
        onehot = sb("onehot", [P, CHUNKS, 2, COLS], f32r)
        vecs = sb("vecs", [P, COLS, VECS])
        dense_rows = vecs[:, :, :].rearrange("p b n -> p (b n)")[:, 0:TILES * D].rearrange("p (t d) -> p t d", d=D)
        products_all = sb("products", [P, 2, N_PER, P])
        products = products_all[0:N_PER, :, :, :]
        table_raw = products_all[:, :, :, :].rearrange("p s m b -> p (s m b)")[:, 0:RAW_SLOTS * CHUNKS * D] \
            .rearrange("p (k d) -> p k d", k=RAW_SLOTS)
        packed = sb("packed", [P, NPAIRCHUNKS, COLS])
        w1_dense = sb("w1_dense", [P, H1])
        w1_tail = sb("w1_tail", [P, H1])
        w1_pairs = sb("w1_pairs", [P, NPAIRCHUNKS, H1])
        w2_sb = sb("w2_sb", [P, HC1, H2])
        small_rows = sb("small_rows", [HC1 + 2 * HC2, P])
        small = sb("small", [P, HC1 + 2 * HC2])
        hidden1 = sb("hidden1", [P, HC1, COLS])
        hidden2 = sb("hidden2", [P, HC2, COLS])
        y = sb("y", [P, TILES])

        bank_t = [bank(f"bank_t{k}") for k in range(2)]
        bank_g = [bank(f"bank_g{k}") for k in range(2)]
        bank_m = [bank(f"bank_m{k}") for k in range(MBANKS)]

        s_ident0, s_ident, s_iota, s_consts = sem("s_ident0"), sem("s_ident"), sem("s_iota"), sem("s_consts")
        s_ids, s_dense, s_small = sem("s_ids"), sem("s_dense"), sem("s_small")
        s_raw = [sem(f"s_raw{k}") for k in range(RAW_SLOTS)]
        s_w1d, s_w = sem("s_w1d"), sem("s_w")
        s_ids_f = sem("s_ids_f")
        s_ids_t, s_scratch = sem("s_ids_t"), sem("s_scratch")
        s_zero = sem("s_zero")
        s_setup = sem("s_setup")
        s_setup_act = sem("s_setup_act")
        s_hi, s_lo = sem("s_hi"), sem("s_lo")
        s_w1sum = sem("s_w1sum")
        s_refill = sem("s_refill")
        s_gids = sem("s_gids")
        s_gath = [[sem(f"s_gath{s}_{g}") for g in range(NGROUPS)] for s in range(2)]
        s_spread = sem("s_spread")
        s_onehot = sem("s_onehot")
        s_sel = sem("s_sel")
        s_t = sem("s_t")
        s_t_act, s_t_dve = sem("s_t_act"), sem("s_t_dve")
        s_g = sem("s_g")
        s_g_act, s_g_dve = sem("s_g_act"), sem("s_g_dve")
        s_pack = [sem(f"s_pack{s}") for s in range(2)]
        s_pack_last = [[sem(f"s_pack_last{s}_{k}") for k in range(NPAIRCHUNKS)] for s in range(2)]
        s_mlp = sem("s_mlp")
        s_m_act = sem("s_m_act")
        s_out = sem("s_out")

        block = ctx.enter_context(nc.Block())

        def use_of(i, what):
            if isinstance(i, int) and i == 0:
                return int(what[-1])
            return i * len(USES) + (USES.index(what) - MLP_USES)

        def bank_of(i, what):
            first = isinstance(i, int) and i == 0
            return bank_m[(int(what[-1]) if first else USES.index(what)) % MBANKS]

        LAST_USE = len(USES) * PAIRS - MLP_USES

        def cols_of(s):
            return slice(s * P, (s + 1) * P)

        @block.sync
        def _(sp):
            sp.dma_start(ids_all[:, :, :], ids.rearrange("(p t) f -> p t f", t=TILES)).then_inc(s_ids, 16)

            def load_table(k):
                src = tables[SELECTED[k] - 1].rearrange("(p c) d -> p (c d)", c=CHUNKS)
                if k >= RAW_SLOTS:
                    sp.wait_ge(s_hi, k - RAW_SLOTS + 1)
                    sp.wait_ge(s_lo, k - RAW_SLOTS + 1)
                lead = SEL_P // 16 * 16
                sp.dma_start(table_raw[0:lead, k % RAW_SLOTS, :], src[0:lead, :]).then_inc(s_raw[k % RAW_SLOTS], 16)
                sp.dma_start(table_raw[lead:SEL_P, k % RAW_SLOTS, :], src[lead:SEL_P, :]).then_inc(s_raw[k % RAW_SLOTS], 16)

            def load_spread(i):
                if isinstance(i, int):
                    src = ids_scratch[i * 2 * NSEL:(i + 1) * 2 * NSEL, :]
                else:
                    src = ids_scratch[bass.ds(i * (2 * NSEL), 2 * NSEL), :]
                sp.dma_start(ids_spread[:, :, :, :].rearrange("p s k b -> p (s k b)"),
                             src.rearrange("(a r) b -> a (r b)", a=1).to_broadcast([P, COLS * NSEL])) \
                    .then_inc(s_spread, 16)

            load_table(0)
            sp.wait_ge(s_ids_t, 1)
            sp.dma_start(ids_scratch[:, :], ids_sel_t[:, :]).then_inc(s_scratch, 16)
            sp.wait_ge(s_scratch, 16)
            load_spread(0)
            for k in range(4, NSEL):
                load_table(k)
            sp.dma_start(w1_dense[:, :], w1[0:D, :]).then_inc(s_w1d, 16)
            sp.dma_start(w1_tail[:, :], w1[D + VECS * N_PER // 2:, :]).then_inc(s_w1d, 16)
            sp.dma_start(w2_sb[:, :, :], w2.rearrange("(k p) n -> p k n", p=P)).then_inc(s_w, 16)
            sp.wait_ge(s_zero, 1)
            for n, (k, row, at, count) in enumerate(weight_rows()):
                if n == SPREAD_AT:
                    sp.wait_ge(s_onehot, SEL_STEPS)
                    load_spread(1)
                sp.dma_start(w1_pairs[row:row + count, k, :], w1[at:at + count, :]).then_inc(s_w, 16)

            def pack(i, s, first, last):
                t = i * 2 + s
                if not first and s == 0:
                    sp.wait_ge(s_mlp, i * MLP_USES + (HC1 - MLP_USES))
                sp.wait_ge(s_g_act, t * 2 + 2)
                sp.wait_ge(s_g_dve, t * 2 + 2)
                for k, row, (n0, n1, m0, m1) in PLACED:
                    sp.dma_start(packed[row:row + (n1 - n0) * (m1 - m0), k, cols_of(s)],
                                 products[n0:n1, s, m0 - 1:m1 - 1, :]) \
                        .then_inc(s_pack_last[s][k] if last else s_pack[s], 16)

            def iteration(i, first, last):
                if not first and not last:
                    sp.wait_ge(s_onehot, i * SEL_STEPS + SEL_STEPS)
                    load_spread(i + 1)
                for s in range(2):
                    pack(i, s, first, last)

            iteration(0, True, False)
            with sp.Fori(1, PAIRS - 1) as i:
                iteration(i, False, False)
            iteration(PAIRS - 1, False, True)
            sp.wait_ge(s_m_act, LAST_USE + 2 * TILE_USES)
            sp.dma_start(out.rearrange("(p t) o -> p (t o)", t=TILES), y[:, :]).then_inc(s_out, 16)
            sp.wait_ge(s_out, 16)

        @block.gpsimd
        def _(pool):
            pool.memset(ident[:, :], 0.0).then_inc(s_ident0, 1)
            pool.iota(row_number_i[:, :], pattern=[[1, CHUNKS]], base=0, channel_multiplier=CHUNKS).then_inc(s_iota, 1)
            pool.wait_ge(s_ident0, 1)
            pool.affine_select(out=ident[:, :], in_=ident[:, :], compare_op=ALU.not_equal, fill=1.0,
                               base=0, pattern=[[-1, P]], channel_multiplier=1).then_inc(s_ident, 1)
            pool.wait_ge(s_ids, 16)
            pool.tensor_copy(gather_ids[:, 0, :], ids_all[:, 0, :]).then_inc(s_gids, 1)

            def gather_tile(i, s, first, last):
                t = i * 2 + s
                pool.wait_ge(s_gids, t + 1)
                for g, (n0, step, count) in enumerate(GROUPS):
                    if not first:
                        pool.wait_ge(s_t, t * NGROUPS + (g + 1 - 2 * NGROUPS))
                        pool.sem_inc(s_refill, 1)
                    for j in range(count):
                        f = n0 + j * step - 1
                        pool.indirect_dma_start(
                            out=gathered[:, s, SLOT_OF_GROUP[g] + j, :], out_offset=None, in_=tables[f][:, :],
                            in_offset=bass.IndirectOffsetOnAxis(ap=gather_ids[:, s, f:f + 1], axis=0),
                            bounds_check=TABLE_ROWS[f] - 1, oob_is_err=False).then_inc(s_gath[s][g], 16)
                    if g == 1 and not (last and s == 1):
                        if not (first and s == 0):
                            for h in range(NGROUPS):
                                pool.wait_ge(s_gath[1 - s][h], (i + s) * (16 * GROUPS[h][2]))
                        pool.wait_ge(s_ids, 16)
                        nxt = ids_all[:, t + 1, :] if first or last else \
                            ids_all[:, bass.ds(t + 1, 1), :].rearrange("p a f -> p (a f)")
                        pool.tensor_copy(gather_ids[:, 1 - s, :], nxt).then_inc(s_gids, 1)

            def gather_pair(i, first, last):
                for s in range(2):
                    gather_tile(i, s, first, last)

            gather_pair(0, True, False)
            with pool.Fori(1, PAIRS - 1) as i:
                gather_pair(i, False, False)
            gather_pair(PAIRS - 1, False, True)

        @block.tensor
        def _(pe):
            def setup_round(r, parts):
                if r == 2:
                    pe.wait_ge(s_ids_t, 1)
                elif r > 2:
                    pe.wait_ge(s_setup_act, r - 2)
                for dst, src, idn in parts:
                    last = nc.tensor.transpose(dst, src, idn)
                last.then_inc(s_setup, 1)

            pe.wait_ge(s_ident, 1)
            pe.wait_ge(s_ids_f, 1)
            setup_round(0, [(bank_t[0][:, 0:P], ids_sel[:, :, :].rearrange("p t k -> p (t k)"), ident[:, :])])
            pe.wait_ge(s_dense, 16)
            for r in range(1, 5):
                setup_round(r, [(bank_t[r % 2][:, q * P:(q + 1) * P], dense_rows[:, 4 * (r - 1) + q, :], ident[:, :])
                                for q in range(4)])
            pe.wait_ge(s_small, 48)
            ns = HC1 + 2 * HC2
            setup_round(5, [(bank_t[1][:, 0:ns], small_rows[:, :], ident[0:ns, 0:ns])])

            def select(i, q, first):
                for h in range(2):
                    if not first or 2 * q + h >= MBANKS:
                        pe.wait_ge(s_m_act, use_of(i, f"table{2 * q + h}") - (MBANKS - 1))
                if first:
                    pe.wait_ge(s_hi, 2 * q + 2)
                    pe.wait_ge(s_lo, 2 * q + 2)
                for c in range(CHUNKS):
                    pe.wait_ge(s_onehot, i * SEL_STEPS + (q * CHUNKS + c + 1))
                    for h in range(2):
                        for part in (table_hi, table_lo):
                            last = nc.tensor.matmul(bank_of(i, f"table{2 * q + h}")[:, 0:COLS],
                                                    part[0:SEL_P, 2 * q + h, c * D:(c + 1) * D],
                                                    onehot[0:SEL_P, c, h, :],
                                                    start=part is table_hi and c == 0,
                                                    stop=part is table_lo and c == CHUNKS - 1)
                    last.then_inc(s_sel, 1)

            def hidden1_part(c, dst, dense_cols, cols):
                nc.tensor.matmul(dst, w1_dense[:, c * P:(c + 1) * P], dense_cols, start=True, stop=False)
                for k, rows in enumerate(CHUNK_SIZES):
                    last = nc.tensor.matmul(dst, w1_pairs[0:rows, k, c * P:(c + 1) * P], packed[0:rows, k, cols],
                                            start=False, stop=k == NPAIRCHUNKS - 1)
                last.then_inc(s_mlp, 1)

            def hidden2_part(c, dst, cols, stored):
                for k in range(HC1):
                    if c == 0:
                        pe.wait_ge(s_m_act, stored(k))
                    last = nc.tensor.matmul(dst, w2_sb[:, k, c * P:(c + 1) * P], hidden1[:, k, cols],
                                            start=k == 0, stop=k == HC1 - 1)
                last.then_inc(s_mlp, 1)

            def out_part(s, dst):
                for k in range(HC2):
                    col = HC1 + HC2 + k
                    last = nc.tensor.matmul(dst, hidden2[:, k, cols_of(s)], small[:, col:col + 1],
                                            start=k == 0, stop=k == HC2 - 1)
                last.then_inc(s_mlp, 1)

            def tower_step(i, what):
                use = use_of(i, what)
                kind, c = what[:-1], int(what[-1])
                dst = bank_of(i, what)
                if what == "hidden1_0":
                    for s in range(2):
                        pe.wait_ge(s_pack[s], i * PACKS)
                if what == "out0":
                    pe.wait_ge(s_m_act, use_of(i, "hidden2_1") + 1)
                else:
                    pe.wait_ge(s_m_act, use - (MBANKS - 1))
                if kind == "hidden1_":
                    if isinstance(i, int):
                        dense_cols = dense_t[:, (i - 1) * COLS:i * COLS]
                    else:
                        dense_cols = dense_t[:, bass.ds(i * COLS - COLS, COLS)]
                    hidden1_part(c, dst[:, 0:COLS], dense_cols, slice(0, COLS))
                elif kind == "hidden2_":
                    hidden2_part(c, dst[:, 0:COLS], slice(0, COLS), lambda k: use_of(i, f"hidden1_{k}") + 1)
                else:
                    out_part(c, dst[:, 0:1])

            def last_tower(s):
                use = LAST_USE + s * TILE_USES
                t = TILES - 2 + s
                banks = [bank_m[(use + j) % MBANKS] for j in range(TILE_USES)]
                for c in range(HC1):
                    pe.wait_ge(s_m_act, use + c - (MBANKS - 1))
                    nc.tensor.matmul(banks[c][:, 0:P], w1_dense[:, c * P:(c + 1) * P],
                                     dense_t[:, t * P:(t + 1) * P], start=True, stop=False)
                for k, rows in enumerate(CHUNK_SIZES):
                    pe.wait_ge(s_pack_last[s][k], 16 * len(RECTANGLES[k]))
                    for c in range(HC1):
                        last = nc.tensor.matmul(banks[c][:, 0:P], w1_pairs[0:rows, k, c * P:(c + 1) * P],
                                                packed[0:rows, k, cols_of(s)], start=False,
                                                stop=k == NPAIRCHUNKS - 1)
                        if k == NPAIRCHUNKS - 1:
                            last.then_inc(s_mlp, 1)
                for c in range(HC2):
                    hidden2_part(c, banks[HC1 + c][:, 0:P], cols_of(s), lambda k: use + max(k, c) + 1)
                pe.wait_ge(s_m_act, use + HC1 + HC2)
                out_part(s, banks[HC1 + HC2][:, 0:1])

            def transpose_group(i, s, g, first):
                count = GROUPS[g][2]
                u = s * NGROUPS + g
                if first and u < 2:
                    pe.wait_ge(s_setup_act, 4 + u)
                else:
                    pe.wait_ge((s_t_act, s_t_dve)[u % 2], i * NGROUPS + u // 2)
                pe.wait_ge(s_gath[s][g], i * (16 * count) + 16 * count)
                for j in range(count):
                    last = nc.tensor.transpose(bank_t[u % 2][:, j * P:(j + 1) * P],
                                               gathered[:, s, SLOT_OF_GROUP[g] + j, :], ident[:, :])
                last.then_inc(s_t, 1)

            def multiply_half(i, s, h, first):
                if h == 0:
                    pe.wait_ge(s_t_act, i * NGROUPS + (3, 5)[s])
                    pe.wait_ge(s_t_dve, i * NGROUPS + (2, 5)[s])
                    if s == 0:
                        pe.wait_ge(s_m_act, use_of(i, f"table{NSEL - 1}") + 1)
                if not (first and s == 0):
                    pe.wait_ge(s_g_act, i * 4 + (2 * s + h - 1))
                    pe.wait_ge(s_g_dve, i * 4 + (2 * s + h - 1))
                for r in range(GRAM_ROWS):
                    for j in range(4):
                        b = s * P + h * 64 + j * GRAM_ROWS + r
                        last = nc.tensor.matmul(
                            bank_g[h][32 * j:32 * j + N_PER, r * N_PER:(r + 1) * N_PER],
                            vecs[:, b, 0:N_PER], vecs[:, b, 1:VECS], start=True, stop=True)
                last.then_inc(s_g, 1)

            def iteration(i, first, last):
                for step in STEPS:
                    if step.startswith("select"):
                        select(i, int(step[-1]), first)
                    elif step.startswith("group"):
                        transpose_group(i, int(step[-2]), int(step[-1]), first)
                    elif step.startswith("products"):
                        multiply_half(i, int(step[-2]), int(step[-1]), first)
                    elif not first:
                        tower_step(i, step)

            iteration(0, True, False)
            pe.wait_ge(s_w, 16 * (len(list(weight_rows())) + 1))
            pe.wait_ge(s_w1sum, 1)
            with pe.Fori(1, PAIRS - 1) as i:
                iteration(i, False, False)
            iteration(PAIRS - 1, False, True)
            last_tower(0)
            last_tower(1)

        @block.scalar
        def _(act):
            def store(dst, src):
                return nc.scalar.activation(dst, src, ACT.Copy)

            act.wait_ge(s_iota, 1)
            store(hidden1[:, 0, 0:1], row_number_i[:, 0:1])
            lead = SEL_P // 16 * 16
            for k in range(1, 4):
                src = tables[SELECTED[k] - 1].rearrange("(p c) d -> p (c d)", c=CHUNKS)
                act.dma_start(table_raw[0:lead, k, :], src[0:lead, :]).then_inc(s_raw[k], 16)
                act.dma_start(table_raw[lead:SEL_P, k, :], src[lead:SEL_P, :]).then_inc(s_raw[k], 16)
                if k == 1:
                    act.dma_start(dense_rows[:, :, :], dense.rearrange("(p t) d -> p t d", t=TILES)).then_inc(s_dense, 16)
            act.dma_start(small_rows[0:HC1, :], b1.rearrange("(c p) -> c p", p=P)).then_inc(s_small, 16)
            act.dma_start(small_rows[HC1:HC1 + HC2, :], b2.rearrange("(c p) -> c p", p=P)).then_inc(s_small, 16)
            act.dma_start(small_rows[HC1 + HC2:HC1 + 2 * HC2, :],
                          w3.rearrange("(c p) o -> c (p o)", p=P)).then_inc(s_small, 16)

            def split_hi(k):
                act.wait_ge(s_raw[k % RAW_SLOTS], 32 * (k // RAW_SLOTS + 1))
                store(table_hi[0:SEL_P, k, :], table_raw[0:SEL_P, k % RAW_SLOTS, :]).then_inc(s_hi, 1)

            def store_selected(i, q):
                act.wait_ge(s_sel, i * SEL_STEPS + (q + 1) * CHUNKS)
                for k in (2 * q, 2 * q + 1):
                    store(vecs[:, :, SELECTED[k]], bank_of(i, f"table{k}")[:, 0:COLS]).then_inc(s_m_act, 1)

            def relu(dst, src, col):
                nc.scalar.activation(dst, src, ACT.Relu, bias=small[:, col:col + 1]).then_inc(s_m_act, 1)

            def tower_step(i, what):
                c = int(what[-1])
                src = bank_of(i, what)
                at = [w for w in USES if not w.startswith("table")].index(what)
                act.wait_ge(s_mlp, i * MLP_USES + (at + 1 - MLP_USES))
                if what.startswith("hidden1"):
                    relu(hidden1[:, c, :], src[:, 0:COLS], c)
                elif what.startswith("hidden2"):
                    relu(hidden2[:, c, :], src[:, 0:COLS], HC1 + c)
                else:
                    dst = y[:, 2 * i - 2 + c:2 * i - 1 + c] if isinstance(i, int) else y[:, bass.ds(2 * i + (c - 2), 1)]
                    store(dst, src[:, 0:1]).then_inc(s_m_act, 1)

            def last_tower(s):
                use = LAST_USE + s * TILE_USES
                done = (PAIRS - 1) * MLP_USES + s * TILE_USES
                for c in range(HC1):
                    act.wait_ge(s_mlp, done + c + 1)
                    relu(hidden1[:, c, cols_of(s)], bank_m[(use + c) % MBANKS][:, 0:P], c)
                for c in range(HC2):
                    act.wait_ge(s_mlp, done + HC1 + c + 1)
                    relu(hidden2[:, c, cols_of(s)], bank_m[(use + HC1 + c) % MBANKS][:, 0:P], HC1 + c)
                act.wait_ge(s_mlp, done + TILE_USES)
                t = TILES - 2 + s
                store(y[:, t:t + 1], bank_m[(use + HC1 + HC2) % MBANKS][:, 0:1]).then_inc(s_m_act, 1)

            def store_group(i, s, g):
                u = s * NGROUPS + g
                n0, step, count = GROUPS[g]
                act.wait_ge(s_t, i * (2 * NGROUPS) + (u + 1))
                if g == 0:
                    store_dense(i, s)
                store(vecs[:, cols_of(s), n0:n0 + step * (count - 1) + 1:step].rearrange("p b n -> p n b"),
                      bank_t[0][:, 0:count * P].rearrange("p (n b) -> p n b", n=count)).then_inc(s_t_act, 1)

            def store_dense(i, s):
                if isinstance(i, int):
                    src = dense_t[:, (2 * i + s) * P:(2 * i + s + 1) * P]
                else:
                    src = dense_t[:, bass.ds(i * COLS + s * P, P)]
                store(vecs[:, cols_of(s), 0], src)

            def store_products(i, s, h, first):
                if not first and h == 0:
                    act.wait_ge(s_pack[s], i * PACKS)
                act.wait_ge(s_g, i * 4 + (2 * s + h + 1))
                for j in (0, 1):
                    b = h * 64 + j * GRAM_ROWS
                    last = store(products[:, s, :, b:b + GRAM_ROWS],
                                 bank_g[h][32 * j:32 * j + N_PER, 0:GRAM_ROWS * N_PER]
                                 .rearrange("p (r m) -> p m r", r=GRAM_ROWS))
                last.then_inc(s_g_act, 1)

            def iteration(i, first, last):
                for step in STEPS:
                    if step.startswith("select"):
                        q = int(step[-1])
                        if first and q + 2 < BANKS_SEL:
                            split_hi(2 * q + 4)
                            split_hi(2 * q + 5)
                        store_selected(i, q)
                    elif step.startswith("group"):
                        s, g = int(step[-2]), int(step[-1])
                        if (s * NGROUPS + g) % 2 == 0:
                            store_group(i, s, g)
                    elif step.startswith("products"):
                        store_products(i, int(step[-2]), int(step[-1]), first)
                    elif not first:
                        tower_step(i, step)

            split_hi(0)
            split_hi(1)
            for r in range(1, 5):
                act.wait_ge(s_setup, r + 1)
                store(dense_t[:, (r - 1) * 512:r * 512], bank_t[r % 2][:, :]).then_inc(s_setup_act, 1)
            act.wait_ge(s_setup, 6)
            store(small[:, :], bank_t[1][:, 0:HC1 + 2 * HC2]).then_inc(s_setup_act, 1)
            split_hi(2)
            split_hi(3)
            iteration(0, True, False)
            with act.Fori(1, PAIRS - 1) as i:
                iteration(i, False, False)
            iteration(PAIRS - 1, False, True)
            last_tower(0)
            last_tower(1)

        @block.vector
        def _(dve):
            dve.wait_ge(s_ids, 16)
            k = 0
            while k < NSEL:
                run = 1
                while k + run < NSEL and SELECTED[k + run] == SELECTED[k] + run:
                    run += 1
                last = nc.vector.tensor_copy(ids_sel[:, :, k:k + run],
                                             ids_all[:, :, SELECTED[k] - 1:SELECTED[k] - 1 + run])
                k += run
            last.then_inc(s_ids_f, 1)
            dve.wait_ge(s_setup, 1)
            nc.vector.tensor_copy(ids_sel_t[:, :], bank_t[0][:, 0:P]).then_inc(s_ids_t, 1)
            nc.vector.memset(w1_pairs[:, :, :], 0.0).then_inc(s_zero, 1)
            dve.wait_ge(s_iota, 1)
            nc.vector.tensor_copy(row_number[:, :], row_number_i[:, :]).then_inc(s_consts, 1)
            dve.wait_ge(s_consts, 1)

            def split_lo(k):
                dve.wait_ge(s_hi, k + 1)
                nc.vector.tensor_tensor(table_lo[0:SEL_P, k, :], table_raw[0:SEL_P, k % RAW_SLOTS, :],
                                        table_hi[0:SEL_P, k, :].bitcast(f32), ALU.subtract).then_inc(s_lo, 1)

            def build_onehot(i, q):
                dve.wait_ge(s_spread, i * 16 + 16)
                for c in range(CHUNKS):
                    if not (isinstance(i, int) and i == 0 and q == 0):
                        dve.wait_ge(s_sel, i * SEL_STEPS + ((q - 1) * CHUNKS + c + 1))
                    nc.vector.tensor_scalar(onehot[0:SEL_P, c, :, :].rearrange("p k (s b) -> p k s b", s=2),
                                            ids_spread[0:SEL_P, :, 2 * q:2 * q + 2, :].rearrange("p s k b -> p k s b"),
                                            row_number[0:SEL_P, c:c + 1], None, ALU.is_equal).then_inc(s_onehot, 1)

            def store_group(i, s, g):
                u = s * NGROUPS + g
                n0, step, count = GROUPS[g]
                dve.wait_ge(s_t, i * (2 * NGROUPS) + (u + 1))
                if g == 0:
                    if isinstance(i, int):
                        src = dense_t[:, (2 * i + s) * P:(2 * i + s + 1) * P]
                    else:
                        src = dense_t[:, bass.ds(i * COLS + s * P, P)]
                    nc.vector.tensor_copy(vecs[:, cols_of(s), 0], src)
                nc.vector.tensor_copy(
                    vecs[:, cols_of(s), n0:n0 + step * (count - 1) + 1:step].rearrange("p b n -> p n b"),
                    bank_t[1][:, 0:count * P].rearrange("p (n b) -> p n b", n=count)).then_inc(s_t_dve, 1)

            def store_products(i, s, h, first):
                if not first and h == 0:
                    dve.wait_ge(s_pack[s], i * PACKS)
                dve.wait_ge(s_g, i * 4 + (2 * s + h + 1))
                for j in (2, 3):
                    b = h * 64 + j * GRAM_ROWS
                    last = nc.vector.tensor_copy(products[:, s, :, b:b + GRAM_ROWS],
                                 bank_g[h][32 * j:32 * j + N_PER, 0:GRAM_ROWS * N_PER]
                                 .rearrange("p (r m) -> p m r", r=GRAM_ROWS))
                last.then_inc(s_g_dve, 1)

            def iteration(i, first, last):
                for step in STEPS:
                    if step.startswith("select"):
                        q = int(step[-1])
                        if q + 1 < BANKS_SEL:
                            if first:
                                split_lo(2 * q + 2)
                                split_lo(2 * q + 3)
                            build_onehot(i, q + 1)
                    elif step.startswith("group"):
                        s, g = int(step[-2]), int(step[-1])
                        if (s * NGROUPS + g) % 2 == 1:
                            store_group(i, s, g)
                    elif step.startswith("products"):
                        store_products(i, int(step[-2]), int(step[-1]), first)
                    if step == NEXT_ONEHOT and not last:
                        build_onehot(i + 1, 0)

            for k in range(2):
                split_lo(k)
            build_onehot(0, 0)
            dve.wait_ge(s_setup_act, 4)
            iteration(0, True, False)
            dve.wait_ge(s_w1d, 32)
            nc.vector.tensor_tensor(w1_dense[:, :], w1_dense[:, :], w1_tail[:, :], ALU.add).then_inc(s_w1sum, 1)
            with dve.Fori(1, PAIRS - 1) as i:
                iteration(i, False, False)
            iteration(PAIRS - 1, False, True)


_INS = ['r_dense_proj', 'ids'] + [f'tbl_{f}' for f in range(FEATURES)] + ['W_top1', 'b_top1', 'W_top2', 'b_top2', 'W_top3']


def kernel(**inputs):
    import numpy as np
    from concourse import bacc
    from concourse.bass_utils import run_bass_kernel_spmd

    nc = bacc.Bacc("TRN2", target_bir_lowering=False, num_devices=1)
    arrays, aps = {}, {}
    for name in _INS:
        a = np.ascontiguousarray(inputs[name])
        arrays[f"in_{name}"] = a
        aps[name] = nc.dram_tensor(f"in_{name}", a.shape, mybir.dt.from_np(a.dtype), kind="ExternalInput").ap()
    out = nc.dram_tensor("out_y", (BATCH, 1), mybir.dt.float32, kind="ExternalOutput").ap()
    ids_scratch = nc.dram_tensor("ids_scratch", (TILES * NSEL, P), mybir.dt.float16, kind="Internal").ap()
    dlrm_tower(nc, aps['r_dense_proj'], aps['ids'], [aps[f'tbl_{f}'] for f in range(FEATURES)],
               aps['W_top1'], aps['b_top1'], aps['W_top2'], aps['b_top2'], aps['W_top3'], ids_scratch, out)
    r = run_bass_kernel_spmd(nc, [arrays], core_ids=[0])
    return r.results[0]["out_y"]
```

```python
import concourse.bass as bass
from concourse import mybir
from contextlib import ExitStack

P = 128
TABLE_ROWS = [12500, 12500, 125000, 1000, 12500, 12500, 12500, 1250, 12500, 1250, 1250, 12500, 1000,
              1000, 1000, 1250, 1000, 1000, 1000, 1000, 1000, 1250, 1250, 1250, 12500, 1250]
BATCH, D, H1, H2 = 2048, 128, 512, 256
FEATURES = len(TABLE_ROWS)
VECS = FEATURES + 1
TILES = BATCH // P
PAIRS = TILES // 2
COLS = 2 * P

SELECTED = [4, 13, 14, 15, 17, 18, 19, 20, 21]
SELECT_ROWS = 1000
CHUNKS = 8
SEL_P = SELECT_ROWS // CHUNKS
NSEL = len(SELECTED)
RAW_SLOTS = 6
SELECTIONS = [[k for k in (q, q + 1) if k < NSEL] for q in range(0, NSEL, 2)]
ID_ROWS = [min(P, TILES * NSEL - r) for r in range(0, TILES * NSEL, P)]
SEL_STEPS = len(SELECTIONS) * CHUNKS
GROUPS = [(1, 1, 3), (5, 1, 4), (9, 1, 4), (22, 1, 4), (16, 10, 2)]
NGROUPS = len(GROUPS)
SLOT_OF_GROUP = [sum(n for _, _, n in GROUPS[:g]) for g in range(NGROUPS)]
NGATHER = sum(n for _, _, n in GROUPS)

N_PER = VECS - 1
RECTANGLES = [[(0, 8, 11, 27)],
              [(8, 17, 17, 27), (0, 4, 4, 11), (0, 3, 1, 4)],
              [(17, 22, 22, 27), (8, 12, 12, 17), (4, 8, 8, 11), (4, 7, 5, 8), (8, 11, 9, 12),
               (12, 16, 13, 17), (17, 21, 18, 22), (22, 26, 23, 27)]]
PLACED = []
CHUNK_SIZES = []
for _k, _rectangles in enumerate(RECTANGLES):
    _row = 0
    for _n0, _n1, _m0, _m1 in _rectangles:
        PLACED.append((_k, _row, (_n0, _n1, _m0, _m1)))
        _row += (_n1 - _n0) * (_m1 - _m0)
    CHUNK_SIZES.append(_row)
NPAIRCHUNKS = len(CHUNK_SIZES)
POOL_PLACED = (5, 7, 9, 11)
assert all(PLACED[n][0] == NPAIRCHUNKS - 1 for n in POOL_PLACED)
PACKS = 16 * len(PLACED)
HC1, HC2 = H1 // P, H2 // P
GRAM_ROWS = 16

STEPS = ["select0", "group00", "select1", "group01", "select2", "group02", "split", "select3", "hidden1_0", "select4",
         "group03", "group04", "hidden1_1", "products00", "group10", "hidden1_2", "group11", "products01", "group12",
         "group13", "hidden1_3", "group14", "hidden2_0", "products10", "hidden2_1", "products11", "out"]
NEXT_ONEHOT = "hidden2_0"
SPREAD_AT = 40
MBANKS = 4
FIRST_STEPS = ["select0", "group00", "select1", "group01", "select2", "group02", "select3", "group03",
               "group04", "select4", "group10", "products00", "group11", "group12", "products01", "group13",
               "group14", "hidden2_0", "products10", "products11"]
LAST_STEPS = [step for step in STEPS if step not in ("hidden2_1", "out")] + ["hidden2_1", "out"]


def uses_of(steps):
    uses = []
    for step in steps:
        if step.startswith("select"):
            uses += [f"table{k}" for k in SELECTIONS[int(step[-1])]]
        elif step[:5] not in ("group", "produ", "split"):
            uses.append(step)
    return uses


USES = uses_of(STEPS)
TOWER_USES = HC1 + HC2 + 1


def pair_row(n, m):
    return D + n * N_PER - n * (n - 1) // 2 + (m - n - 1)


def weight_rows():
    for k, row, (n0, n1, m0, m1) in PLACED:
        for n in range(n0, n1):
            m = max(m0, n + 1)
            yield k, row + (n - n0) * (m1 - m0) + (m - m0), pair_row(n, m), m1 - m


def dlrm_tower(nc, dense, ids, tables, w1, b1, w2, b2, w3, ids_scratch, out):
    f32, f32r, f16, i32 = mybir.dt.float32, mybir.dt.float32r, mybir.dt.float16, mybir.dt.int32
    ALU = mybir.AluOpType
    ACT = mybir.ActivationFunctionType
    ctx = ExitStack()
    with ctx:
        def sb(name, shape, dt=f32):
            return ctx.enter_context(nc.sbuf_tensor(name, shape, dt))

        def bank(name):
            return ctx.enter_context(nc.psum_tensor(name, [P, 512], f32))

        def sem(name):
            return ctx.enter_context(nc.semaphore(name))

        ident = sb("ident", [P, P])
        row_number_i = sb("row_number_i", [P, CHUNKS], i32)
        row_number = sb("row_number", [P, CHUNKS])
        ids_all = sb("ids_all", [P, TILES, FEATURES], i32)
        ids_spread = sb("ids_spread", [P, 2, NSEL, P], f16)
        gather_ids = sb("gather_ids", [P, 2, FEATURES], i32)
        gathered = sb("gathered", [P, 2, NGATHER, D])
        dense_t = sb("dense_t", [P, BATCH])
        table_hi = sb("table_hi", [P, NSEL, CHUNKS * D], f32r)
        table_lo = sb("table_lo", [P, NSEL, CHUNKS * D], f32r)
        onehot = sb("onehot", [P, CHUNKS, 2, COLS], f32r)
        vecs = sb("vecs", [P, COLS, VECS])
        dense_rows = vecs[:, :, :].rearrange("p b n -> p (b n)")[:, 0:TILES * D].rearrange("p (t d) -> p t d", d=D)
        products_all = sb("products", [P, N_PER, 2, P])
        products = products_all[0:N_PER, :, :, :]
        table_raw = products_all[:, :, :, :].rearrange("p m s b -> p (m s b)")[:, 0:RAW_SLOTS * CHUNKS * D] \
            .rearrange("p (k d) -> p k d", k=RAW_SLOTS)
        packed = sb("packed", [P, NPAIRCHUNKS, COLS])
        ids_sel = packed[:, 0, 0:TILES * NSEL].rearrange("p (t k) -> p t k", k=NSEL)
        ids_sel_t = packed[:, 1, 0:P].bitcast(f16).rearrange("p (a b) -> p a b", b=P)
        packed_hi = sb("packed_hi", [P, NPAIRCHUNKS, COLS], f32r)
        packed_lo = sb("packed_lo", [P, NPAIRCHUNKS, COLS], f32r)
        w1_hi = sb("w1_hi", [P, NPAIRCHUNKS, H1], f32r)
        w1_lo = sb("w1_lo", [P, NPAIRCHUNKS, H1], f32r)
        w1_dense = sb("w1_dense", [P, H1])
        w2_sb = sb("w2_sb", [P, HC1, H2])
        small_rows = sb("small_rows", [HC1 + 2 * HC2, P])
        small = sb("small", [P, HC1 + 2 * HC2])
        hidden = sb("hidden", [P, HC1 + HC2, COLS])
        hidden1, hidden2 = hidden[:, 0:HC1, :], hidden[:, HC1:HC1 + HC2, :]
        w1_pairs = hidden[:, :, :].rearrange("p c b -> p (c b)").rearrange("p (k n) -> p k n", n=H1)
        w1_tail = packed[:, 0:H1 // COLS, :].rearrange("p c b -> p (c b)")
        y = sb("y", [P, TILES])

        bank_t = [bank(f"bank_t{k}") for k in range(2)]
        bank_g = [bank(f"bank_g{k}") for k in range(2)]
        bank_m = [bank(f"bank_m{k}") for k in range(MBANKS)]

        s_ident0, s_ident, s_iota, s_consts = sem("s_ident0"), sem("s_ident"), sem("s_iota"), sem("s_consts")
        s_ids, s_dense, s_small = sem("s_ids"), sem("s_dense"), sem("s_small")
        s_raw = [sem(f"s_raw{k}") for k in range(RAW_SLOTS)]
        s_w1d, s_w = sem("s_w1d"), sem("s_w")
        s_ids_f = sem("s_ids_f")
        s_ids_t, s_scratch = sem("s_ids_t"), sem("s_scratch")
        s_zero = sem("s_zero")
        s_setup = sem("s_setup")
        s_setup_act = sem("s_setup_act")
        s_hi, s_lo = sem("s_hi"), sem("s_lo")
        s_w1sum = sem("s_w1sum")
        s_w1_hi, s_w1_lo = sem("s_w1_hi"), sem("s_w1_lo")
        s_packed_hi, s_packed_lo = sem("s_packed_hi"), sem("s_packed_lo")
        s_refill = sem("s_refill")
        s_gids = sem("s_gids")
        s_gath = [[sem(f"s_gath{s}_{g}") for g in range(NGROUPS)] for s in range(2)]
        s_spread = sem("s_spread")
        s_onehot = sem("s_onehot")
        s_sel = sem("s_sel")
        s_t = sem("s_t")
        s_t_act, s_t_dve = sem("s_t_act"), sem("s_t_dve")
        s_g = sem("s_g")
        s_g_act, s_g_dve = sem("s_g_act"), sem("s_g_dve")
        s_pack = sem("s_pack")
        s_pack_last = [[sem(f"s_pack_last{s}_{k}") for k in range(NPAIRCHUNKS)] for s in range(2)]
        s_pack_pool = [sem(f"s_pack_pool{s}") for s in range(2)]
        s_mlp = sem("s_mlp")
        s_m_act = sem("s_m_act")
        s_out = sem("s_out")

        block = ctx.enter_context(nc.Block())

        def use_of(i, what):
            if isinstance(i, int) and i == 0:
                return int(what[len("table"):])
            return i * len(USES) + (USES.index(what) - TOWER_USES)

        assert len(USES) % MBANKS == 0

        def bank_of(i, what):
            first = isinstance(i, int) and i == 0
            return bank_m[(use_of(0, what) if first else USES.index(what) - TOWER_USES) % MBANKS]

        LAST_USE = len(USES) * PAIRS - TOWER_USES

        def split_of(s, k):
            return PAIRS - 1 + s * NPAIRCHUNKS + k

        def cols_of(s):
            return slice(s * P, (s + 1) * P)

        @block.sync
        def _(sp):
            sp.dma_start(ids_all[:, :, :], ids.rearrange("(p t) f -> p t f", t=TILES)).then_inc(s_ids, 16)

            def load_table(k):
                src = tables[SELECTED[k] - 1].rearrange("(p c) d -> p (c d)", c=CHUNKS)
                if k >= RAW_SLOTS:
                    sp.wait_ge(s_hi, k - RAW_SLOTS + 1)
                    sp.wait_ge(s_lo, k - RAW_SLOTS + 1)
                lead = SEL_P // 16 * 16
                sp.dma_start(table_raw[0:lead, k % RAW_SLOTS, :], src[0:lead, :]).then_inc(s_raw[k % RAW_SLOTS], 16)
                sp.dma_start(table_raw[lead:SEL_P, k % RAW_SLOTS, :], src[lead:SEL_P, :]).then_inc(s_raw[k % RAW_SLOTS], 16)

            def load_spread(i):
                if isinstance(i, int):
                    src = ids_scratch[i * 2 * NSEL:(i + 1) * 2 * NSEL, :]
                else:
                    src = ids_scratch[bass.ds(i * (2 * NSEL), 2 * NSEL), :]
                sp.dma_start(ids_spread[:, :, :, :].rearrange("p s k b -> p (s k b)"),
                             src.rearrange("(a r) b -> a (r b)", a=1).to_broadcast([P, COLS * NSEL])) \
                    .then_inc(s_spread, 16)

            load_table(0)
            sp.wait_ge(s_ids_t, 1)
            for r, rows in enumerate(ID_ROWS):
                sp.dma_start(ids_scratch[r * P:r * P + rows, :], ids_sel_t[0:rows, r, :]).then_inc(s_scratch, 16)
            sp.wait_ge(s_scratch, 16 * len(ID_ROWS))
            load_spread(0)
            for k in range(4, NSEL):
                load_table(k)
            sp.dma_start(w1_dense[:, :], w1[0:D, :]).then_inc(s_w1d, 16)
            sp.dma_start(w1_tail, w1[D + VECS * N_PER // 2:, :]).then_inc(s_w1d, 16)
            sp.dma_start(w2_sb[:, :, :], w2.rearrange("(k p) n -> p k n", p=P)).then_inc(s_w, 16)
            sp.wait_ge(s_zero, 1)
            for n, (k, row, at, count) in enumerate(weight_rows()):
                if n == SPREAD_AT:
                    sp.wait_ge(s_onehot, SEL_STEPS)
                    load_spread(1)
                sp.dma_start(w1_pairs[row:row + count, k, :], w1[at:at + count, :]).then_inc(s_w, 16)

            def pack(i, first):
                if not first:
                    sp.wait_ge(s_mlp, i * TOWER_USES + (HC1 - TOWER_USES))
                sp.wait_ge(s_g_act, i * 4 + 4)
                sp.wait_ge(s_g_dve, i * 4 + 4)
                for k, row, (n0, n1, m0, m1) in PLACED:
                    sp.dma_start(packed[row:row + (n1 - n0) * (m1 - m0), k, :],
                                 products[n0:n1, m0 - 1:m1 - 1, :, :].rearrange("n m s b -> n m (s b)")) \
                        .then_inc(s_pack, 16)

            def pack_last(s):
                t = TILES - 2 + s
                if s == 0:
                    sp.wait_ge(s_mlp, (PAIRS - 2) * TOWER_USES + HC1)
                sp.wait_ge(s_g_act, t * 2 + 2)
                sp.wait_ge(s_g_dve, t * 2 + 2)
                for n, (k, row, (n0, n1, m0, m1)) in enumerate(PLACED):
                    if n not in POOL_PLACED:
                        sp.dma_start(packed[row:row + (n1 - n0) * (m1 - m0), k, cols_of(s)],
                                     products[n0:n1, m0 - 1:m1 - 1, s, :]).then_inc(s_pack_last[s][k], 16)

            def iteration(i, first):
                if not first:
                    sp.wait_ge(s_onehot, i * SEL_STEPS + SEL_STEPS)
                    load_spread(i + 1)
                pack(i, first)

            iteration(0, True)
            with sp.Fori(1, PAIRS - 1) as i:
                iteration(i, False)
            pack_last(0)
            pack_last(1)
            sp.wait_ge(s_m_act, LAST_USE + TOWER_USES)
            sp.dma_start(out.rearrange("(p t) o -> p (t o)", t=TILES), y[:, :]).then_inc(s_out, 16)
            sp.wait_ge(s_out, 16)

        @block.gpsimd
        def _(pool):
            pool.memset(ident[:, :], 0.0).then_inc(s_ident0, 1)
            pool.iota(row_number_i[:, :], pattern=[[1, CHUNKS]], base=0, channel_multiplier=CHUNKS).then_inc(s_iota, 1)
            pool.wait_ge(s_ident0, 1)
            pool.affine_select(out=ident[:, :], in_=ident[:, :], compare_op=ALU.not_equal, fill=1.0,
                               base=0, pattern=[[-1, P]], channel_multiplier=1).then_inc(s_ident, 1)

            def gather_tile(i, s, first):
                t = i * 2 + s
                if first:
                    pool.wait_ge(s_ids, 16)
                else:
                    pool.wait_ge(s_gids, t - 1)
                for g, (n0, step, count) in enumerate(GROUPS):
                    if not first:
                        pool.wait_ge(s_t, t * NGROUPS + (g + 1 - 2 * NGROUPS))
                        pool.sem_inc(s_refill, 1)
                    for j in range(count):
                        f = n0 + j * step - 1
                        index = ids_all[:, t, f:f + 1] if first else gather_ids[:, s, f:f + 1]
                        pool.indirect_dma_start(
                            out=gathered[:, s, SLOT_OF_GROUP[g] + j, :], out_offset=None, in_=tables[f][:, :],
                            in_offset=bass.IndirectOffsetOnAxis(ap=index, axis=0),
                            bounds_check=TABLE_ROWS[f] - 1, oob_is_err=False).then_inc(s_gath[s][g], 16)
            for s in range(2):
                gather_tile(0, s, True)
            with pool.Fori(1, PAIRS) as i:
                for s in range(2):
                    gather_tile(i, s, False)
            for s in range(2):
                t = TILES - 2 + s
                if s == 0:
                    pool.wait_ge(s_mlp, (PAIRS - 2) * TOWER_USES + HC1)
                pool.wait_ge(s_g_act, t * 2 + 2)
                pool.wait_ge(s_g_dve, t * 2 + 2)
                for k, row, (n0, n1, m0, m1) in [PLACED[n] for n in POOL_PLACED]:
                    pool.dma_start(packed[row:row + (n1 - n0) * (m1 - m0), k, cols_of(s)],
                                   products[n0:n1, m0 - 1:m1 - 1, s, :]).then_inc(s_pack_pool[s], 16)

        @block.tensor
        def _(pe):
            def setup_round(r, parts):
                if r == 2:
                    pe.wait_ge(s_ids_t, 1)
                elif r > 2:
                    pe.wait_ge(s_setup_act, r - 2)
                for dst, src, idn in parts:
                    last = nc.tensor.transpose(dst, src, idn)
                last.then_inc(s_setup, 1)

            pe.wait_ge(s_ident, 1)
            pe.wait_ge(s_ids_f, 1)
            id_columns = ids_sel[:, :, :].rearrange("p t k -> p (t k)")
            setup_round(0, [(bank_t[0][0:rows, r * P:(r + 1) * P], id_columns[:, r * P:r * P + rows], ident[:, :])
                            for r, rows in enumerate(ID_ROWS)])
            def transpose_dense():
                pe.wait_ge(s_dense, 16)
                for r in range(1, 5):
                    setup_round(r, [(bank_t[r % 2][:, q * P:(q + 1) * P], dense_rows[:, 4 * (r - 1) + q, :],
                                     ident[:, :]) for q in range(4)])
                pe.wait_ge(s_small, 48)
                ns = HC1 + 2 * HC2
                setup_round(5, [(bank_t[1][:, 0:ns], small_rows[:, :], ident[0:ns, 0:ns])])

            def select(i, q, first):
                for k in SELECTIONS[q]:
                    if not first or k >= MBANKS:
                        pe.wait_ge(s_m_act, use_of(i, f"table{k}") - (MBANKS - 1))
                if first:
                    pe.wait_ge(s_hi, SELECTIONS[q][-1] + 1)
                    pe.wait_ge(s_lo, SELECTIONS[q][-1] + 1)
                for c in range(CHUNKS):
                    pe.wait_ge(s_onehot, i * SEL_STEPS + (q * CHUNKS + c + 1))
                    for h, k in enumerate(SELECTIONS[q]):
                        for part in (table_hi, table_lo):
                            last = nc.tensor.matmul(bank_of(i, f"table{k}")[:, 0:COLS],
                                                    part[0:SEL_P, k, c * D:(c + 1) * D],
                                                    onehot[0:SEL_P, c, h, :],
                                                    start=part is table_hi and c == 0,
                                                    stop=part is table_lo and c == CHUNKS - 1)
                    last.then_inc(s_sel, 1)

            def hidden1_dense(c, dst, dense_cols):
                nc.tensor.matmul(dst, w1_dense[:, c * P:(c + 1) * P], dense_cols, start=True, stop=False)

            def hidden1_chunk(c, k, dst, cols):
                rows = CHUNK_SIZES[k]
                for n, (w, x) in enumerate(((w1_hi, packed_hi), (w1_lo, packed_hi), (w1_hi, packed_lo))):
                    last = nc.tensor.matmul(dst, w[0:rows, k, c * P:(c + 1) * P], x[0:rows, k, cols],
                                            start=False, stop=k == NPAIRCHUNKS - 1 and n == 2)
                return last

            def hidden2_part(c, dst, cols, stored):
                for k in range(HC1):
                    if c == 0:
                        pe.wait_ge(s_m_act, stored(k))
                    last = nc.tensor.matmul(dst, w2_sb[:, k, c * P:(c + 1) * P], hidden1[:, k, cols],
                                            start=k == 0, stop=k == HC1 - 1)
                last.then_inc(s_mlp, 1)

            def out_part(s, dst, signal):
                for k in range(HC2):
                    col = HC1 + HC2 + k
                    last = nc.tensor.matmul(dst, hidden2[:, k, cols_of(s)], small[:, col:col + 1],
                                            start=k == 0, stop=k == HC2 - 1)
                if signal:
                    last.then_inc(s_mlp, 1)

            def tower_step(i, what):
                use = use_of(i, what)
                dst = bank_of(i, what)
                if what == "hidden1_0":
                    pe.wait_ge(s_w1_lo, 1)
                    pe.wait_ge(s_packed_lo, i)
                if what == "out":
                    pe.wait_ge(s_m_act, use_of(i, "hidden2_1") + 1)
                else:
                    pe.wait_ge(s_m_act, use - (MBANKS - 1))
                if what.startswith("hidden1"):
                    if isinstance(i, int):
                        dense_cols = dense_t[:, (i - 1) * COLS:i * COLS]
                    else:
                        dense_cols = dense_t[:, bass.ds(i * COLS - COLS, COLS)]
                    hidden1_dense(int(what[-1]), dst[:, 0:COLS], dense_cols)
                    for k in range(NPAIRCHUNKS):
                        last = hidden1_chunk(int(what[-1]), k, dst[:, 0:COLS], slice(0, COLS))
                    last.then_inc(s_mlp, 1)
                elif what.startswith("hidden2"):
                    hidden2_part(int(what[-1]), dst[:, 0:COLS], slice(0, COLS), lambda k: use_of(i, f"hidden1_{k}") + 1)
                else:
                    for s in range(2):
                        out_part(s, dst[:, s:s + 1], s == 1)

            def last_tower():
                banks = [bank_m[(LAST_USE + j) % MBANKS] for j in range(TOWER_USES)]
                for c in range(HC1):
                    pe.wait_ge(s_m_act, LAST_USE + c - (MBANKS - 1))
                    nc.tensor.matmul(banks[c][:, 0:COLS], w1_dense[:, c * P:(c + 1) * P],
                                     dense_t[:, (PAIRS - 1) * COLS:], start=True, stop=False)
                for k in range(NPAIRCHUNKS):
                    pe.wait_ge(s_packed_lo, split_of(1, k) + 1)
                    for c in range(HC1):
                        last = hidden1_chunk(c, k, banks[c][:, 0:COLS], slice(0, COLS))
                        if k == NPAIRCHUNKS - 1:
                            last.then_inc(s_mlp, 1)
                for k in range(HC1):
                    for c in range(HC2):
                        pe.wait_ge(s_m_act, LAST_USE + max(k, c) + 1)
                        last = nc.tensor.matmul(banks[HC1 + c][:, 0:COLS], w2_sb[:, k, c * P:(c + 1) * P],
                                                hidden1[:, k, :], start=k == 0, stop=k == HC1 - 1)
                        if k == HC1 - 1:
                            last.then_inc(s_mlp, 1)
                pe.wait_ge(s_m_act, LAST_USE + HC1 + HC2)
                for s in range(2):
                    out_part(s, banks[HC1 + HC2][:, s:s + 1], s == 1)

            def transpose_group(i, s, g, first):
                count = GROUPS[g][2]
                u = s * NGROUPS + g
                if first and u < 2:
                    pe.wait_ge(s_setup_act, 4 + u)
                else:
                    pe.wait_ge((s_t_act, s_t_dve)[u % 2], i * NGROUPS + u // 2)
                pe.wait_ge(s_gath[s][g], i * (16 * count) + 16 * count)
                for j in range(count):
                    last = nc.tensor.transpose(bank_t[u % 2][:, j * P:(j + 1) * P],
                                               gathered[:, s, SLOT_OF_GROUP[g] + j, :], ident[:, :])
                last.then_inc(s_t, 1)

            def multiply_half(i, s, h, first):
                if h == 0:
                    pe.wait_ge(s_t_act, i * NGROUPS + (3, 5)[s])
                    pe.wait_ge(s_t_dve, i * NGROUPS + (2, 5)[s])
                    if s == 0:
                        pe.wait_ge(s_m_act, use_of(i, f"table{NSEL - 1}") + 1)
                if not (first and s == 0):
                    pe.wait_ge(s_g_act, i * 4 + (2 * s + h - 1))
                    pe.wait_ge(s_g_dve, i * 4 + (2 * s + h - 1))
                for r in range(GRAM_ROWS):
                    for j in range(4):
                        b = s * P + h * 64 + j * GRAM_ROWS + r
                        last = nc.tensor.matmul(
                            bank_g[h][32 * j:32 * j + N_PER, r * N_PER:(r + 1) * N_PER],
                            vecs[:, b, 0:N_PER], vecs[:, b, 1:VECS], start=True, stop=True)
                last.then_inc(s_g, 1)

            def iteration(i, first, last):
                for step in (FIRST_STEPS if first else LAST_STEPS if last else STEPS):
                    if step.startswith("select"):
                        select(i, int(step[-1]), first)
                        if first and step == "select0":
                            transpose_dense()
                    elif step.startswith("group"):
                        transpose_group(i, int(step[-2]), int(step[-1]), first)
                    elif step.startswith("products"):
                        multiply_half(i, int(step[-2]), int(step[-1]), first)
                    elif not first and not step.startswith("split"):
                        tower_step(i, step)

            iteration(0, True, False)
            with pe.Fori(1, PAIRS - 1) as i:
                iteration(i, False, False)
            iteration(PAIRS - 1, False, True)
            last_tower()

        @block.scalar
        def _(act):
            def store(dst, src):
                return nc.scalar.activation(dst, src, ACT.Copy)

            act.wait_ge(s_iota, 1)
            store(y[:, 0:1], row_number_i[:, 0:1])
            def load_table(k):
                lead = SEL_P // 16 * 16
                src = tables[SELECTED[k] - 1].rearrange("(p c) d -> p (c d)", c=CHUNKS)
                act.dma_start(table_raw[0:lead, k, :], src[0:lead, :]).then_inc(s_raw[k], 16)
                act.dma_start(table_raw[lead:SEL_P, k, :], src[lead:SEL_P, :]).then_inc(s_raw[k], 16)

            load_table(1)
            load_table(2)

            def split_hi(k):
                act.wait_ge(s_raw[k % RAW_SLOTS], 32 * (k // RAW_SLOTS + 1))
                store(table_hi[0:SEL_P, k, :], table_raw[0:SEL_P, k % RAW_SLOTS, :]).then_inc(s_hi, 1)

            def split_packed(i):
                act.wait_ge(s_pack, i * PACKS)
                for k, rows in enumerate(CHUNK_SIZES):
                    last = store(packed_hi[0:rows, k, :], packed[0:rows, k, :])
                last.then_inc(s_packed_hi, 1)

            def split_packed_last(s):
                for k, rows in enumerate(CHUNK_SIZES):
                    by_pool = len(POOL_PLACED) if k == NPAIRCHUNKS - 1 else 0
                    act.wait_ge(s_pack_last[s][k], 16 * (len(RECTANGLES[k]) - by_pool))
                    if by_pool:
                        act.wait_ge(s_pack_pool[s], 16 * by_pool)
                    store(packed_hi[0:rows, k, cols_of(s)], packed[0:rows, k, cols_of(s)]).then_inc(s_packed_hi, 1)

            def store_selected(i, q):
                act.wait_ge(s_sel, i * SEL_STEPS + (q + 1) * CHUNKS)
                for k in SELECTIONS[q]:
                    store(vecs[:, :, SELECTED[k]], bank_of(i, f"table{k}")[:, 0:COLS]).then_inc(s_m_act, 1)

            def relu(dst, src, col):
                nc.scalar.activation(dst, src, ACT.Relu, bias=small[:, col:col + 1]).then_inc(s_m_act, 1)

            def tower_step(i, what):
                src = bank_of(i, what)
                at = [w for w in USES if not w.startswith("table")].index(what)
                act.wait_ge(s_mlp, i * TOWER_USES + (at + 1 - TOWER_USES))
                if what.startswith("hidden1"):
                    c = int(what[-1])
                    relu(hidden1[:, c, :], src[:, 0:COLS], c)
                elif what.startswith("hidden2"):
                    c = int(what[-1])
                    relu(hidden2[:, c, :], src[:, 0:COLS], HC1 + c)
                else:
                    dst = y[:, 2 * i - 2:2 * i] if isinstance(i, int) else y[:, bass.ds(2 * i - 2, 2)]
                    store(dst, src[:, 0:2]).then_inc(s_m_act, 1)

            def last_tower():
                done = (PAIRS - 1) * TOWER_USES
                for c in range(HC1):
                    act.wait_ge(s_mlp, done + c + 1)
                    relu(hidden1[:, c, :], bank_m[(LAST_USE + c) % MBANKS][:, 0:COLS], c)
                for c in range(HC2):
                    act.wait_ge(s_mlp, done + HC1 + c + 1)
                    relu(hidden2[:, c, :], bank_m[(LAST_USE + HC1 + c) % MBANKS][:, 0:COLS], HC1 + c)
                act.wait_ge(s_mlp, done + TOWER_USES)
                store(y[:, TILES - 2:], bank_m[(LAST_USE + HC1 + HC2) % MBANKS][:, 0:2]).then_inc(s_m_act, 1)

            def store_group(i, s, g):
                u = s * NGROUPS + g
                n0, step, count = GROUPS[g]
                act.wait_ge(s_t, i * (2 * NGROUPS) + (u + 1))
                if g == 0:
                    store_dense(i, s)
                store(vecs[:, cols_of(s), n0:n0 + step * (count - 1) + 1:step].rearrange("p b n -> p n b"),
                      bank_t[0][:, 0:count * P].rearrange("p (n b) -> p n b", n=count)).then_inc(s_t_act, 1)

            def store_dense(i, s):
                if isinstance(i, int):
                    src = dense_t[:, (2 * i + s) * P:(2 * i + s + 1) * P]
                else:
                    src = dense_t[:, bass.ds(i * COLS + s * P, P)]
                store(vecs[:, cols_of(s), 0], src)

            def store_products(i, s, h, first):
                if not first and s == 0 and h == 0:
                    act.wait_ge(s_pack, i * PACKS)
                act.wait_ge(s_g, i * 4 + (2 * s + h + 1))
                for j in (0, 1):
                    b = h * 64 + j * GRAM_ROWS
                    last = store(products[:, :, s, b:b + GRAM_ROWS],
                                 bank_g[h][32 * j:32 * j + N_PER, 0:GRAM_ROWS * N_PER]
                                 .rearrange("p (r m) -> p m r", r=GRAM_ROWS))
                last.then_inc(s_g_act, 1)

            def iteration(i, first, last):
                for step in (FIRST_STEPS if first else LAST_STEPS if last else STEPS):
                    if step.startswith("select"):
                        q = int(step[-1])
                        if first and q + 2 < len(SELECTIONS):
                            for k in SELECTIONS[q + 2]:
                                if k > 5:
                                    split_hi(k)
                        store_selected(i, q)
                    elif step.startswith("group"):
                        s, g = int(step[-2]), int(step[-1])
                        if (s * NGROUPS + g) % 2 == 0:
                            store_group(i, s, g)
                    elif step.startswith("products"):
                        store_products(i, int(step[-2]), int(step[-1]), first)
                    elif step == "split":
                        if not first:
                            split_packed(i)
                    elif not first:
                        tower_step(i, step)

            for k in range(3):
                split_hi(k)
            act.wait_ge(s_scratch, 16 * len(ID_ROWS))
            load_table(3)
            act.dma_start(dense_rows[:, :, :], dense.rearrange("(p t) d -> p t d", t=TILES)).then_inc(s_dense, 16)
            act.dma_start(small_rows[0:HC1, :], b1.rearrange("(c p) -> c p", p=P)).then_inc(s_small, 16)
            act.dma_start(small_rows[HC1:HC1 + HC2, :], b2.rearrange("(c p) -> c p", p=P)).then_inc(s_small, 16)
            act.dma_start(small_rows[HC1 + HC2:HC1 + 2 * HC2, :],
                          w3.rearrange("(c p) o -> c (p o)", p=P)).then_inc(s_small, 16)
            split_hi(3)
            split_hi(4)
            for r in range(1, 5):
                act.wait_ge(s_setup, r + 1)
                store(dense_t[:, (r - 1) * 512:r * 512], bank_t[r % 2][:, :]).then_inc(s_setup_act, 1)
                if r == 2:
                    split_hi(5)
            act.wait_ge(s_setup, 6)
            store(small[:, :], bank_t[1][:, 0:HC1 + 2 * HC2]).then_inc(s_setup_act, 1)
            iteration(0, True, False)
            act.wait_ge(s_w, 16 * (len(list(weight_rows())) + 1))
            store(w1_hi[:, :, :], w1_pairs).then_inc(s_w1_hi, 1)
            with act.Fori(1, PAIRS - 1) as i:
                iteration(i, False, False)
            iteration(PAIRS - 1, False, True)
            split_packed_last(0)
            split_packed_last(1)
            last_tower()

        @block.vector
        def _(dve):
            dve.wait_ge(s_ids, 16)
            k = 0
            while k < NSEL:
                run = 1
                while k + run < NSEL and SELECTED[k + run] == SELECTED[k] + run:
                    run += 1
                last = nc.vector.tensor_copy(ids_sel[:, :, k:k + run],
                                             ids_all[:, :, SELECTED[k] - 1:SELECTED[k] - 1 + run])
                k += run
            last.then_inc(s_ids_f, 1)
            dve.wait_ge(s_setup, 1)
            for r, rows in enumerate(ID_ROWS):
                last = nc.vector.tensor_copy(ids_sel_t[0:rows, r, :], bank_t[0][0:rows, r * P:(r + 1) * P])
            last.then_inc(s_ids_t, 1)
            nc.vector.memset(w1_pairs[:, :, :], 0.0).then_inc(s_zero, 1)
            dve.wait_ge(s_iota, 1)
            nc.vector.tensor_copy(row_number[:, :], row_number_i[:, :]).then_inc(s_consts, 1)
            dve.wait_ge(s_consts, 1)

            def split_lo(k):
                dve.wait_ge(s_hi, k + 1)
                nc.vector.tensor_tensor(table_lo[0:SEL_P, k, :], table_raw[0:SEL_P, k % RAW_SLOTS, :],
                                        table_hi[0:SEL_P, k, :].bitcast(f32), ALU.subtract).then_inc(s_lo, 1)

            def build_onehot(i, q):
                dve.wait_ge(s_spread, i * 16 + 16)
                for c in range(CHUNKS):
                    if not (isinstance(i, int) and i == 0 and q == 0):
                        dve.wait_ge(s_sel, i * SEL_STEPS + ((q - 1) * CHUNKS + c + 1))
                    n, k = len(SELECTIONS[q]), SELECTIONS[q][0]
                    nc.vector.tensor_scalar(onehot[0:SEL_P, c, 0:n, :].rearrange("p k (s b) -> p k s b", s=2),
                                            ids_spread[0:SEL_P, :, k:k + n, :].rearrange("p s k b -> p k s b"),
                                            row_number[0:SEL_P, c:c + 1], None, ALU.is_equal).then_inc(s_onehot, 1)

            def store_group(i, s, g):
                u = s * NGROUPS + g
                n0, step, count = GROUPS[g]
                dve.wait_ge(s_t, i * (2 * NGROUPS) + (u + 1))
                if g == 0:
                    if isinstance(i, int) and i == 0:
                        dve.wait_ge(s_setup_act, 4)
                    if isinstance(i, int):
                        src = dense_t[:, (2 * i + s) * P:(2 * i + s + 1) * P]
                    else:
                        src = dense_t[:, bass.ds(i * COLS + s * P, P)]
                    nc.vector.tensor_copy(vecs[:, cols_of(s), 0], src)
                nc.vector.tensor_copy(
                    vecs[:, cols_of(s), n0:n0 + step * (count - 1) + 1:step].rearrange("p b n -> p n b"),
                    bank_t[1][:, 0:count * P].rearrange("p (n b) -> p n b", n=count)).then_inc(s_t_dve, 1)

            def split_packed(i):
                dve.wait_ge(s_packed_hi, i)
                for k, rows in enumerate(CHUNK_SIZES):
                    last = nc.vector.tensor_tensor(packed_lo[0:rows, k, :], packed[0:rows, k, :],
                                                   packed_hi[0:rows, k, :].bitcast(f32), ALU.subtract)
                last.then_inc(s_packed_lo, 1)

            def split_packed_last(s):
                for k, rows in enumerate(CHUNK_SIZES):
                    dve.wait_ge(s_packed_hi, split_of(s, k) + 1)
                    nc.vector.tensor_tensor(packed_lo[0:rows, k, cols_of(s)], packed[0:rows, k, cols_of(s)],
                                            packed_hi[0:rows, k, cols_of(s)].bitcast(f32),
                                            ALU.subtract).then_inc(s_packed_lo, 1)

            def copy_indices(i, s):
                if isinstance(i, int):
                    src = ids_all[:, i * 2 + s, :]
                else:
                    src = ids_all[:, bass.ds(i * 2 + s, 1), :].rearrange("p a f -> p (a f)")
                nc.vector.tensor_copy(gather_ids[:, s, :], src).then_inc(s_gids, 1)

            def store_products(i, s, h, first):
                if not first and s == 0 and h == 0:
                    dve.wait_ge(s_pack, i * PACKS)
                dve.wait_ge(s_g, i * 4 + (2 * s + h + 1))
                for j in (2, 3):
                    b = h * 64 + j * GRAM_ROWS
                    last = nc.vector.tensor_copy(products[:, :, s, b:b + GRAM_ROWS],
                                 bank_g[h][32 * j:32 * j + N_PER, 0:GRAM_ROWS * N_PER]
                                 .rearrange("p (r m) -> p m r", r=GRAM_ROWS))
                last.then_inc(s_g_dve, 1)

            def iteration(i, first, last):
                for step in (FIRST_STEPS if first else LAST_STEPS if last else STEPS):
                    if step.startswith("select"):
                        q = int(step[-1])
                        if q + 1 < len(SELECTIONS):
                            if first and q > 0:
                                for k in SELECTIONS[q + 1]:
                                    split_lo(k)
                            build_onehot(i, q + 1)
                            if first and q == 0:
                                split_lo(3)
                    elif step.startswith("group"):
                        s, g = int(step[-2]), int(step[-1])
                        if (s * NGROUPS + g) % 2 == 1:
                            store_group(i, s, g)
                    elif step.startswith("products"):
                        store_products(i, int(step[-2]), int(step[-1]), first)
                    elif step == "split" and not first:
                        split_packed(i)
                    if step in ("group10", "group14") and not last:
                        copy_indices(i + 1, 0 if step == "group10" else 1)
                    if step == "group14" and first:
                        dve.wait_ge(s_w1d, 32)
                        nc.vector.tensor_tensor(w1_dense[:, :], w1_dense[:, :], w1_tail,
                                                ALU.add).then_inc(s_w1sum, 1)
                    if step == NEXT_ONEHOT and not last:
                        build_onehot(i + 1, 0)

            for k in range(3):
                split_lo(k)
            build_onehot(0, 0)
            iteration(0, True, False)
            dve.wait_ge(s_w1_hi, 1)
            nc.vector.tensor_tensor(w1_lo[:, :, :], w1_pairs, w1_hi[:, :, :].bitcast(f32), ALU.subtract) \
                .then_inc(s_w1_lo, 1)
            with dve.Fori(1, PAIRS - 1) as i:
                iteration(i, False, False)
            iteration(PAIRS - 1, False, True)
            split_packed_last(0)
            split_packed_last(1)


_INS = ['r_dense_proj', 'ids'] + [f'tbl_{f}' for f in range(FEATURES)] + ['W_top1', 'b_top1', 'W_top2', 'b_top2', 'W_top3']


def kernel(**inputs):
    import numpy as np
    from concourse import bacc
    from concourse.bass_utils import run_bass_kernel_spmd

    nc = bacc.Bacc("TRN2", target_bir_lowering=False, num_devices=1)
    arrays, aps = {}, {}
    for name in _INS:
        a = np.ascontiguousarray(inputs[name])
        arrays[f"in_{name}"] = a
        aps[name] = nc.dram_tensor(f"in_{name}", a.shape, mybir.dt.from_np(a.dtype), kind="ExternalInput").ap()
    out = nc.dram_tensor("out_y", (BATCH, 1), mybir.dt.float32, kind="ExternalOutput").ap()
    ids_scratch = nc.dram_tensor("ids_scratch", (TILES * NSEL, P), mybir.dt.float16, kind="Internal").ap()
    dlrm_tower(nc, aps['r_dense_proj'], aps['ids'], [aps[f'tbl_{f}'] for f in range(FEATURES)],
               aps['W_top1'], aps['b_top1'], aps['W_top2'], aps['b_top2'], aps['W_top3'], ids_scratch, out)
    r = run_bass_kernel_spmd(nc, [arrays], core_ids=[0])
    return r.results[0]["out_y"]
```
